# Optimizing a Trainium2 kernel written in Bass

```python
import numpy as np
import jax
import jax.numpy as jnp

def _softmax(x, axis=-1):
    return jax.nn.softmax(x, axis=axis)

def _gelu(x):
    return jax.nn.gelu(x, approximate=True)

def _silu(x):
    return jax.nn.silu(x)

def _sigmoid(x):
    return jax.nn.sigmoid(x)

def _layernorm(x, axis=-1, eps=1e-05):
    m = jnp.mean(x, axis=axis, keepdims=True)
    v = jnp.var(x, axis=axis, keepdims=True)
    return (x - m) / jnp.sqrt(v + eps)

def _scatter_add(tgt, idx, src, axis=0):
    return tgt.at[idx].add(src)

def _segment_sum(src, seg, n):
    return jax.ops.segment_sum(src, seg, n)
kernel_name = 'mk_rec_standalone_d1_rec_r8_705aee'

def setup_inputs(seed: int=0):
    np.random.seed(seed)
    _w = jnp.asarray

    def _rec_inputs():
        import jax
        import jax.numpy as jnp
        _rk = jax.random.key(seed)
        r_input = jax.random.randint(jax.random.fold_in(_rk, 1), (512, 200), 23, 149997, jnp.int32)
        return r_input
    r_input = _rec_inputs()

    def _L0_rec_setup():
        import jax, jax.numpy as jnp
        import numpy as np
        NTOKEN = 18750
        NINP = 64
        NHID = 2 * NINP
        NEDGE = 300000
        B, L = (64, 200)

        def gcn_conv(x, W, b, src, dst, n):
            h = x @ W
            deg = jnp.zeros((n,), h.dtype).at[dst].add(1.0) + 1.0
            dinv = jax.lax.rsqrt(deg)
            norm = dinv[src] * dinv[dst]
            agg = jax.ops.segment_sum(h[src] * norm[:, None], dst, num_segments=n)
            return agg + h * (dinv * dinv)[:, None] + b
        key = jax.random.key(seed)
        ks = jax.random.split(key, 8)

        def xavier(k, shape):
            scale = (2.0 / (shape[0] + shape[1])) ** 0.5
            return scale * jax.random.normal(k, shape, jnp.float32)
        emb = xavier(ks[0], (NTOKEN, NINP)).at[0].set(0.0)
        W1 = xavier(ks[1], (NINP, NHID))
        b1 = jnp.zeros((NHID,), jnp.float32)
        W2 = xavier(ks[2], (NHID, NINP))
        b2 = jnp.zeros((NINP,), jnp.float32)
        edge_index = jax.random.randint(ks[3], (2, NEDGE), 0, NTOKEN, dtype=jnp.int32).astype(jnp.int64)
        inp = jax.random.randint(ks[4], (B, L), 0, NTOKEN, dtype=jnp.int32).astype(jnp.int64)
        input_timestamp = jax.random.randint(ks[5], (B, L), 0, 37500, dtype=jnp.int32).astype(jnp.int64)
        return {'emb': emb, 'W1': W1, 'b1': b1, 'W2': W2, 'b2': b2, 'input': inp, 'input_timestamp': input_timestamp, 'edge_index': edge_index}
    _L0_rec_all = _L0_rec_setup()
    _L0_rec_in = {k: v for k, v in _L0_rec_all.items() if k in ('emb', 'W1', 'b1', 'W2', 'b2', 'input_timestamp', 'edge_index')}
    del _L0_rec_all
    return {'r_input': r_input, 'L0_rec_emb': _L0_rec_in['emb'], 'L0_rec_W1': _L0_rec_in['W1'], 'L0_rec_b1': _L0_rec_in['b1'], 'L0_rec_W2': _L0_rec_in['W2'], 'L0_rec_b2': _L0_rec_in['b2'], 'L0_rec_input_timestamp': _L0_rec_in['input_timestamp'], 'L0_rec_edge_index': _L0_rec_in['edge_index']}

def reference(r_input, L0_rec_emb, L0_rec_W1, L0_rec_b1, L0_rec_W2, L0_rec_b2, L0_rec_input_timestamp, L0_rec_edge_index):
    import jax
    import jax.numpy as jnp

    def _L0_rec_ref(emb, W1, b1, W2, b2, input, input_timestamp, edge_index):
        import jax, jax.numpy as jnp
        import numpy as np
        NTOKEN = 18750
        NINP = 64
        NHID = 2 * NINP
        NEDGE = 300000
        B, L = (64, 200)

        def gcn_conv(x, W, b, src, dst, n):
            h = x @ W
            deg = jnp.zeros((n,), h.dtype).at[dst].add(1.0) + 1.0
            dinv = jax.lax.rsqrt(deg)
            norm = dinv[src] * dinv[dst]
            agg = jax.ops.segment_sum(h[src] * norm[:, None], dst, num_segments=n)
            return agg + h * (dinv * dinv)[:, None] + b
        src, dst = (edge_index[0], edge_index[1])
        h = gcn_conv(emb, W1, b1, src, dst, NTOKEN)
        nodes = gcn_conv(h, W2, b2, src, dst, NTOKEN)
        b_, l_ = input.shape
        return nodes[input.reshape(-1)].reshape(b_, l_, NINP)
    y = _L0_rec_ref(L0_rec_emb, L0_rec_W1, L0_rec_b1, L0_rec_W2, L0_rec_b2, r_input, L0_rec_input_timestamp, L0_rec_edge_index)
    return y

_drawn_inputs = setup_inputs


def setup_inputs(seed=0):
    import zlib

    import numpy as np

    out = dict(_drawn_inputs(seed))
    spreads = {'L0_rec_b1': (0.0, 0.1), 'L0_rec_b2': (0.0, 0.1)}
    factors = {'L0_rec_emb': 8.0, 'L0_rec_W1': 8.0}
    for name, (base, spread) in spreads.items():
        noise = np.random.default_rng([zlib.crc32(name.encode()), seed]).standard_normal(out[name].shape)
        drawn = base * np.exp(spread * noise) if base else spread * noise
        out[name] = jnp.asarray(drawn.astype(out[name].dtype))
    for name, factor in factors.items():
        out[name] = (out[name] * factor).astype(out[name].dtype)
    return out
```

```python
from contextlib import ExitStack

import concourse.bass as bass
from concourse import mybir

ALU = mybir.AluOpType
ACT = mybir.ActivationFunctionType
AX = mybir.AxisListType
F32 = mybir.dt.float32
BF16 = mybir.dt.bfloat16
I32 = mybir.dt.int32
I16 = mybir.dt.int16

P = 128
NODES, F, HID, EDGES = 18750, 64, 128, 300000
BATCH, SEQ = 512, 200
REQS = BATCH * SEQ
RT = REQS // P
OG = 20

BLOCKS = -(-NODES // P)
BB = 8
NBATCH = 19
PADB = BB * NBATCH
FULLB = NODES // P
TAIL = NODES - FULLB * P
PARTS = 3
ROW = PARTS * F

CHUNKS, SB = 5, 16
COLS = (1 << SB) // P
ALL = CHUNKS * COLS
EP = 125
EC = EDGES // EP
CE = EC // CHUNKS
OFF = 2
KSHIFT = 15
PADKEY = float(2 ** 127)
TG = 20
HT = TG // 2
GROUPS = -(-(-(-EC * EP // CHUNKS // P)) * CHUNKS // TG)
TILES = GROUPS * TG
W = 2
HB = EC // TG


def gcn_program(nc, r_input, emb, w1, b1, w2, b2, edges, out):
    table = nc.dram_tensor("table", (PADB * P, ROW), BF16, kind="Internal").ap()
    nodes = nc.dram_tensor("nodes", (NODES, F), F32, kind="Internal").ap()

    ctx = ExitStack()
    with ctx:
        def sb(name, shape, dt):
            return ctx.enter_context(nc.sbuf_tensor(name, shape, dt))

        def sem(name):
            return ctx.enter_context(nc.semaphore(name))

        acc = sb("acc", [P, PADB * F], F32)
        acc3 = acc[:, :].rearrange("p (b f) -> p b f", f=F)
        raw = sb("raw", [P, 3 * EC], I32)
        dst_raw, src_raw = raw[0:EP, 0:EC], raw[0:EP, EC:2 * EC]
        dlo = raw[0:EP, 2 * EC:2 * EC + EC // 2].bitcast(BF16)
        dhi = raw[0:EP, 2 * EC + EC // 2:3 * EC].bitcast(BF16)
        skey = raw[:, 0:TILES]
        sidx = sb("sidx", [P, TILES], I32)
        sdst = raw[:, EC:EC + TILES]
        rel = raw[:, 2 * EC:2 * EC + TILES // 2].bitcast(BF16)
        sblk = raw[:, 2 * EC + EC // 2:2 * EC + EC // 2 + TILES // 2].bitcast(BF16)
        k_a = sb("k_a", [P, ALL], F32)
        k_b = sb("k_b", [P, ALL], F32)
        sgn_t = sb("sgn_t", [P, 7, P], BF16)
        sgn_l = sb("sgn_l", [P, SB - 7, COLS], BF16)
        it_i = sb("it_i", [P, COLS], I32)
        it_x = sb("it_x", [P, COLS], I32)
        it_y = sb("it_y", [P, COLS], I32)
        iorep = sb("iorep", [P, W * P, HT], BF16)
        oh = sb("oh", [P, 2, (P + BLOCKS) * HT], BF16)
        ohw = oh[:, 0, 0:W * P * HT].rearrange("p (j t) -> p j t", t=HT)
        ring = sb("ring", [P, TG, ROW], BF16)
        gidx = sb("gidx", [P, TG], I32)
        tab = sb("tab", [P, 2, BB, ROW], BF16)
        res = sb("res", [P, 2, BB * F], F32)
        stage = sb("stage", [P, BB * F], F32)
        zt = sb("zt", [P, BB * F], F32)
        tnode = sb("tnode", [P, BB * F], F32)
        blo = sb("blo", [1, TILES], I16)
        span = sb("span", [1, TILES], I16)
        gspan = sb("gspan", [1, GROUPS], I16)
        dinv = sb("dinv", [P, PADB], F32)
        deg = sb("deg", [P, PADB], F32)
        nwt = sb("nwt", [P, PADB], F32)
        colf = sb("colf", [P, P], F32)
        rowf = sb("rowf", [P, 1], F32)
        ident = sb("ident", [P, P], F32)
        sel = sb("sel", [P, 2, P], BF16)
        zero = sb("zero", [P, BLOCKS], BF16)
        zf = sb("zf", [P, P], F32)
        w1s = sb("w1s", [F, HID], F32)
        w1t = sb("w1t", [HID, P], F32)
        w2s = sb("w2s", [HID, F], F32)
        b1s = sb("b1s", [HID, 1], F32)
        b1r = sb("b1r", [HID, P], F32)
        b2r = sb("b2r", [P, F], F32)
        w12 = sb("w12", [P, P], F32)
        c12 = sb("c12", [P, F], F32)
        req = sb("req", [P, RT], I32)
        oidx = sb("oidx", [P, 2, OG], I32)
        xblk = sb("xblk", [P, PADB], F32)
        xdst = sb("xdst", [P, 1], I32)
        xdsf = sb("xdsf", [P, 1], F32)
        xoh = sb("xoh", [P, P], BF16)

        psum = [ctx.enter_context(nc.psum_tensor(f"ps{i}", [P, 512], F32)) for i in range(8)]

        emb_in = sem("emb_in")
        edge_in = sem("edge_in")
        w_in = sem("w_in")
        req_in = sem("req_in")
        iotas = sem("iotas")
        const = sem("const")
        hist_oh = sem("hist_oh")
        hist_mm = sem("hist_mm")
        step = sem("step")
        deg_ready = sem("deg_ready")
        root = sem("root")
        scaled = sem("scaled")
        part_act = sem("part_act")
        part_pool = sem("part_pool")
        tab_out = [sem(f"tab_out{s}") for s in range(2)]
        stage_done = sem("stage_done")
        k_stage = sem("k_stage")
        tr_l = sem("tr_l")
        tr_t = sem("tr_t")
        ev_l = sem("ev_l")
        ev_t = sem("ev_t")
        prep = sem("prep")
        bc = sem("bc")
        sorted_ready = sem("sorted_ready")
        idx_ready = sem("idx_ready")
        gathered = [sem(f"gathered{u}") for u in range(TG)]
        oh_ready = sem("oh_ready")
        mm_done = sem("mm_done")
        added = sem("added")
        x_oh = sem("x_oh")
        x_mm = sem("x_mm")
        x_chain = sem("x_chain")
        held = sem("held")
        setup_mm = sem("setup_mm")
        node_st = sem("node_st")
        node_tr = sem("node_tr")
        node_zt = sem("node_zt")
        node_mm = sem("node_mm")
        rows_ready = sem("rows_ready")
        nodes_out = sem("nodes_out")
        out_idx = sem("out_idx")
        got = [sem(f"got{s}") for s in range(2)]
        out_done = [sem(f"out_done{s}") for s in range(2)]

        block = ctx.enter_context(nc.Block())

        def batches(eng, body):
            for s in range(2):
                body(s, s, 0)
            with eng.Fori(1, NBATCH // 2) as i:
                for s in range(2):
                    body(i * 2 + s, s, i)
            body(NBATCH - 1, 0, NBATCH // 2)

        FREE_MM, FREE_PS = TG, 4
        NPS = 4

        phases = range(8, SB + 1)
        steps = [("sign", 0, k_b, k_a, 0)]
        turns = []
        turned = []
        done, cur, other = 1, k_a, k_b
        for k in range(1, SB + 1):
            if 1 < k < 8:
                steps.append(("sign", k - 1, cur, other, done))
                done, cur, other = done + 1, other, cur
            for bit in range(k - 1, -1, -1):
                fresh = k >= 8 and bit in (k - 1, 6)
                if fresh:
                    turns.append((done, cur))
                    cur, other = other, cur
                    steps.append(("from_l" if bit == k - 1 else "from_t", k, None, cur, 0))
                    if bit == 6:
                        turned.append(cur)
                stride = 1 << (bit - 7 if bit >= 7 else bit)
                steps.append(("exchange", stride, cur, other, 0 if fresh else done))
                done, cur, other = done + 2, other, cur
        turns.append((done, cur))

        def turn(pe, src, signal):
            for c in range(CHUNKS):
                for q in range(COLS // P):
                    mm = pe.transpose(psum[c][:, q * P:(q + 1) * P],
                                      src[:, c * COLS + q * P:c * COLS + (q + 1) * P], ident[:, :])
                mm.then_inc(signal, 1)

        def load_row(eng, ap, most):
            return nc.values_load_multi_w_load_instructions(
                ap, engines=[eng.engine], min_val=0, max_val=most,
                skip_runtime_bounds_check_because="the rows hold clamped block numbers")[1]

        def wait_if(eng, signal, value):
            if not (isinstance(value, int) and value == 0):
                eng.wait_ge(signal, value)

        def peeled(eng, n, body):
            body(0)
            with eng.Fori(1, n) as i:
                body(i)

        class Count:

            def __init__(self, eng, name):
                self.eng, self.reg = eng, eng.alloc_register(name)
                eng.reg_mov(self.reg, 0)

            def add(self):
                self.eng.reg_add(self.reg, self.reg, 1)

            def value(self):
                return self.eng.snap(self.reg, min_val=0, max_val=1 << 24)

        @block.sync
        def _(sp):
            sp.dma_start(dst_raw, edges[1].rearrange("(p j) -> p j", p=EP)).then_inc(edge_in, 16)
            sp.dma_start(src_raw, edges[0].rearrange("(p j) -> p j", p=EP)).then_inc(edge_in, 16)
            sp.dma_start(w1s[:, :], w1).then_inc(w_in, 16)
            sp.dma_start(w2s[:, :], w2).then_inc(w_in, 16)
            sp.dma_start(b1s[:, :], b1.rearrange("(h a) -> h a", a=1)).then_inc(w_in, 16)
            sp.dma_start(b2r[:, :], b2.rearrange("(a f) -> a f", a=1).to_broadcast([P, F])).then_inc(w_in, 16)
            sp.dma_start(req[:, :], r_input.rearrange("a b -> (a b)").rearrange("(p t) -> p t", p=P)).then_inc(req_in, 16)
            sp.wait_ge(const, 1)
            sp.dma_start(acc3[:, 0:FULLB, :], emb[0:FULLB * P, :].rearrange("(b p) f -> p b f", p=P)).then_inc(emb_in, 16)
            sp.dma_start(acc3[0:TAIL, FULLB, :], emb[FULLB * P:NODES, :]).then_inc(emb_in, 16)

            for layer in range(2):
                def store(g, s, i):
                    sp.wait_ge(part_act, PARTS * (g + 1 + layer * NBATCH))
                    rows = table[bass.ds(g * (BB * P), BB * P), :].rearrange("(b p) f -> p b f", p=P)
                    sp.dma_start(rows, tab[:, s, :, :]).then_inc(tab_out[s], 16)
                batches(sp, store)

            sp.wait_ge(rows_ready, 1)
            sp.dma_start(nodes[0:FULLB * P, :].rearrange("(b p) f -> p b f", p=P), acc3[:, 0:FULLB, :]).then_inc(nodes_out, 16)
            sp.dma_start(nodes[FULLB * P:NODES, :], acc3[0:TAIL, FULLB, :]).then_inc(nodes_out, 16)
            rows = out.rearrange("a b f -> (a b) f").rearrange("(p t) f -> p (t f)", p=P)

            def write(i):
                for s in range(2):
                    sp.wait_ge(got[s], (i + 1) * (16 * OG))
                    sp.dma_start(rows[:, bass.ds((i * 2 + s) * (OG * F), OG * F)],
                                 acc[:, s * OG * F:(s + 1) * OG * F]).then_inc(out_done[s], 16)
            peeled(sp, RT // OG // 2, write)
            for s in range(2):
                sp.wait_ge(out_done[s], 16 * (RT // OG // 2))

        @block.gpsimd
        def _(pool):
            pool.iota(it_i[:, :], pattern=[[1, COLS]], base=0, channel_multiplier=0).then_inc(iotas, 1)
            pool.iota(it_x[:, 0:P], pattern=[[1, P]], base=0, channel_multiplier=P).then_inc(iotas, 1)
            pool.iota(it_y[:, 0:1], pattern=[[1, 1]], base=0, channel_multiplier=1).then_inc(iotas, 1)
            pool.iota(iorep[:, :, :], pattern=[[1, W * P], [0, HT]], base=0, channel_multiplier=0,
                      allow_small_or_imprecise_dtypes=True).then_inc(iotas, 1)

            for layer in range(2):
                def rest(g, s, i):
                    b = g + layer * NBATCH
                    x = acc[:, bass.ds(g * (BB * F), BB * F)].rearrange("p (b f) -> p b f", f=F)
                    r = [res[:, n, :].rearrange("p (b f) -> p b f", f=F) for n in range(2)]
                    pool.wait_ge(part_act, b * PARTS + 1)
                    pool.tensor_tensor(r[0], x, tab[:, s, :, 0:F], ALU.subtract).then_inc(part_pool, 1)
                    pool.wait_ge(part_pool, b * 2 + 1)
                    pool.wait_ge(part_act, b * PARTS + 2)
                    pool.tensor_tensor(r[1], r[0], tab[:, s, :, F:2 * F], ALU.subtract).then_inc(part_pool, 1)
                batches(pool, rest)

                pool.wait_ge(tab_out[0], 16 * (NBATCH // 2 + 1) * (layer + 1))
                pool.wait_ge(tab_out[1], 16 * (NBATCH // 2) * (layer + 1))
                with pool.Fori(0, GROUPS) as i:
                    for u in range(TG):
                        if u % HT == 0:
                            pool.wait_ge(idx_ready, (i + layer * GROUPS) * 2 + (u // HT + 1))
                            pool.sem_inc(held, 1)
                        pool.indirect_dma_start(
                            out=ring[:, u, :], out_offset=None, in_=table,
                            in_offset=bass.IndirectOffsetOnAxis(ap=gidx[:, u:u + 1], axis=0)).then_inc(gathered[u], 16)

            pool.wait_ge(nodes_out, 32)

            def fetch(i):
                for s in range(2):
                    pool.wait_ge(out_idx, i * 2 + (s + 1))
                    wait_if(pool, out_done[s], i * 16)
                    pool.sem_inc(held, 1)
                    for t in range(OG):
                        pool.indirect_dma_start(
                            out=acc[:, (s * OG + t) * F:(s * OG + t + 1) * F], out_offset=None, in_=nodes,
                            in_offset=bass.IndirectOffsetOnAxis(ap=oidx[:, s, t:t + 1], axis=0)).then_inc(got[s], 16)
            peeled(pool, RT // OG // 2, fetch)
            for s in range(2):
                pool.wait_ge(got[s], 16 * OG * (RT // OG // 2))

        @block.scalar
        def _(act):
            act.wait_ge(deg_ready, 1)
            act.activation(nwt[:, :], deg[:, :], ACT.Sqrt).then_inc(root, 1)

            for layer in range(2):
                def parts(g, s, i):
                    b = g + layer * NBATCH
                    x = acc[:, bass.ds(g * (BB * F), BB * F)].rearrange("p (b f) -> p b f", f=F)
                    r = [res[:, n, :].rearrange("p (b f) -> p b f", f=F) for n in range(2)]
                    if layer == 0:
                        act.wait_ge(scaled, 1)
                    else:
                        act.wait_ge(node_st, 1 + g * 3 + 3)
                    if layer == 0:
                        wait_if(act, tab_out[s], i * 16)
                    else:
                        act.wait_ge(tab_out[s], (i + (NBATCH // 2 + 1 - s)) * 16)
                    act.activation(tab[:, s, :, 0:F], x, ACT.Copy).then_inc(part_act, 1)
                    act.wait_ge(part_pool, b * 2 + 1)
                    act.activation(tab[:, s, :, F:2 * F], r[0], ACT.Copy).then_inc(part_act, 1)
                    act.wait_ge(part_pool, b * 2 + 2)
                    act.activation(tab[:, s, :, 2 * F:3 * F], r[1], ACT.Copy).then_inc(part_act, 1)

                if layer == 0:
                    batches(act, parts)
                    for n, dst in enumerate(turned):
                        for c in range(CHUNKS):
                            act.wait_ge(tr_t, n * CHUNKS + c + 1)
                            act.activation(dst[:, c * COLS:(c + 1) * COLS], psum[c][:, 0:COLS], ACT.Copy).then_inc(ev_t, 1)
                else:
                    def nodes_t(g, s, i):
                        act.wait_ge(node_tr, g + 1)
                        act.activation(zt[:, :], psum[5][:, :], ACT.Copy).then_inc(node_zt, 1)
                        parts(g, s, i)
                    batches(act, nodes_t)

                act.wait_ge(sorted_ready, 1)
                with act.Fori(0, GROUPS) as i:
                    for h in range(2):
                        act.wait_ge(mm_done, (i + layer * GROUPS) * TG + (h + 1) * HT)
                        act.copy(gidx[:, h * HT:(h + 1) * HT],
                                 sidx[:, bass.ds(i * TG + h * HT, HT)]).then_inc(idx_ready, 1)


            def indices(i):
                for s in range(2):
                    wait_if(act, got[s], i * (16 * OG))
                    act.copy(oidx[:, s, :], req[:, bass.ds((i * 2 + s) * OG, OG)]).then_inc(out_idx, 1)
            peeled(act, RT // OG // 2, indices)

        @block.tensor
        def _(pe):
            visits = Count(pe, "pe_visits")
            pe.sem_inc(mm_done, FREE_MM)
            pe.sem_inc(hist_mm, 2)
            pe.wait_ge(const, 2)
            pe.wait_ge(w_in, 64)
            pe.transpose(psum[6][:, 0:F], w1s[:, :], ident[0:F, 0:F]).then_inc(setup_mm, 1)
            pe.wait_ge(const, 3)
            pe.matmul(psum[5][:, 0:F], w1t[:, :], w2s[:, :], start=True, stop=True).then_inc(setup_mm, 1)
            pe.matmul(psum[4][:, 0:F], b1r[:, :], w2s[:, :], start=True, stop=True).then_inc(setup_mm, 1)

            pe.matmul(psum[7][:, 0:BLOCKS], sel[:, 0, :], zero[:, :], start=True, stop=False)
            with pe.Fori(0, HB) as i:
                for h in range(2):
                    lane = oh[0:EP, h, 0:P * HT].rearrange("p (j t) -> p j t", t=HT)
                    blk = oh[0:EP, h, P * HT:].rearrange("p (j t) -> p j t", t=HT)
                    pe.wait_ge(hist_oh, i * 4 + (2 * h + 2))
                    for t in range(HT):
                        mm = pe.matmul(psum[7][:, 0:BLOCKS], lane[:, :, t], blk[:, :, t], start=False, stop=False)
                    mm.then_inc(hist_mm, 1)
            pe.matmul(psum[7][:, 0:BLOCKS], sel[:, 0, :], zero[:, :], start=False, stop=True).then_inc(hist_mm, 1)

            for n, (ready, src) in enumerate(turns):
                pe.wait_ge(k_stage, ready)
                if n:
                    pe.wait_ge(ev_l if n % 2 else ev_t, (n + 1) // 2 * CHUNKS)
                turn(pe, src, tr_t if n % 2 else tr_l)

            for e in range(2):
                pe.wait_ge(prep, 1 + 5 * e)
                for c in range(CHUNKS):
                    pe.matmul(psum[c][:, 0:TILES // CHUNKS], sel[:, e, :],
                              sblk[:, c * (TILES // CHUNKS):(c + 1) * (TILES // CHUNKS)],
                              start=True, stop=True).then_inc(bc, 1)

            for layer in range(2):
                pe.wait_ge(sorted_ready, 1)
                with pe.Fori(0, GROUPS) as i:
                    most = pe.value_load(gspan[0:1, bass.ds(i, 1)], min_val=0, max_val=BLOCKS)
                    with pe.If(most >= W):
                        for u in range(TG):
                            pe.wait_ge(gathered[u], (i + (layer * GROUPS + 1)) * 16)
                        pe.sem_inc(held, 1)
                        with pe.Fori(0, TG) as u:
                            s = pe.value_load(span[0:1, bass.ds(i * TG + u, 1)], min_val=0, max_val=BLOCKS)
                            with pe.If(s >= W):
                                with pe.Fori(W, s + 1) as j:
                                    visits.add()
                                    pe.wait_ge(x_oh, visits.value())
                                    for a in range(PARTS):
                                        mm = pe.matmul(psum[4][:, 0:F], xoh[:, :],
                                                       ring[:, :, :].rearrange("p u f -> p (u f)")[:, bass.ds(u * ROW + a * F, F)],
                                                       start=(a == 0), stop=(a == PARTS - 1))
                                    mm.then_inc(x_mm, 1)
                                pe.nop()
                            pe.nop()
                        pe.nop()
                    for u in range(TG):
                        if u % HT == 0:
                            pe.wait_ge(oh_ready, (i + layer * GROUPS) * 2 + (u // HT + 1))
                        pe.wait_ge(gathered[u], (i + (layer * GROUPS + 1)) * 16)
                        pe.wait_ge(added, (i + layer * GROUPS) * TG + (u + 1))
                        for w in range(W):
                            for a in range(PARTS):
                                mm = pe.matmul(psum[u % NPS][:, w * F:(w + 1) * F],
                                               ohw[:, w * P:(w + 1) * P, u % HT], ring[:, u, a * F:(a + 1) * F],
                                               start=(a == 0), stop=(a == PARTS - 1))
                        mm.then_inc(mm_done, 1)
                if layer == 0:
                    def node_rows(g, s, i):
                        pe.wait_ge(node_st, g * 3 + 1 + 1)
                        for q in range(BB // 2):
                            mm = pe.transpose(psum[5][:, q * P:(q + 1) * P], stage[:, q * P:(q + 1) * P], ident[:, :])
                        mm.then_inc(node_tr, 1)
                        pe.wait_ge(node_zt, g + 1)
                        for q in range(BB // 2):
                            mm = pe.matmul(psum[6][:, q * P:(q + 1) * P], zt[:, q * P:(q + 1) * P], w12[:, :],
                                           start=True, stop=True)
                        mm.then_inc(node_mm, 1)
                    batches(pe, node_rows)

        @block.vector
        def _(dve):
            visits = Count(dve, "dve_visits")
            chain = Count(dve, "dve_chain")
            blk_reg = dve.alloc_register("dve_block")
            at = [0]

            def link(ins):
                at[0] += 1
                ins.then_inc(step, 1)
                dve.wait_ge(step, at[0])

            dve.sem_inc(added, FREE_PS)
            link(dve.memset(acc[:, FULLB * F:], 0.0))
            dve.sem_inc(const, 1)

            dve.memset(zero[:, :], 0.0)
            dve.memset(w12[:, :], 0.0)
            dve.memset(zf[:, :], 0.0)
            dve.memset(deg[:, :], 1.0)
            link(dve.memset(k_b[:, :], PADKEY))
            dve.wait_ge(iotas, 4)
            dve.tensor_copy(colf[:, :], it_i[:, 0:P])
            link(dve.tensor_copy(rowf[:, :], it_y[:, 0:1]))
            link(dve.tensor_scalar(ident[:, :], colf[:, :], rowf[:, 0:1], None, ALU.is_equal))
            link(dve.tensor_copy(sel[:, 0, :], ident[:, 0:1].to_broadcast([P, P])))
            link(dve.tensor_copy(sel[:, 1, :], ident[:, P - 1:P].to_broadcast([P, P])))
            link(dve.tensor_scalar(xblk[:, :], it_i[:, 0:PADB], float(P), float(OFF * P), ALU.mult, ALU.add))
            dve.sem_inc(const, 1)
            for k in range(7):
                if k == 0:
                    link(dve.tensor_scalar(k_a[:, 0:P].bitcast(I32), it_x[:, 0:P], 1, 1, ALU.logical_shift_right, ALU.bitwise_and))
                else:
                    link(dve.tensor_scalar(k_a[:, P:2 * P].bitcast(I32), it_x[:, 0:P], k, None, ALU.logical_shift_right))
                    link(dve.tensor_scalar(k_a[:, 0:P].bitcast(I32), it_x[:, 0:P], k + 1, None, ALU.logical_shift_right))
                    link(dve.tensor_tensor(k_a[:, P:2 * P].bitcast(I32), k_a[:, 0:P].bitcast(I32), k_a[:, P:2 * P].bitcast(I32), ALU.bitwise_xor))
                    link(dve.tensor_scalar(k_a[:, 0:P].bitcast(I32), k_a[:, P:2 * P].bitcast(I32), 1, None, ALU.bitwise_and))
                link(dve.tensor_scalar(sgn_t[:, k, :], k_a[:, 0:P].bitcast(I32), -2.0, 1.0, ALU.mult, ALU.add))
            for k in range(7, SB):
                x = k_a[:, 0:COLS].bitcast(I32)
                y = k_a[:, COLS:2 * COLS].bitcast(I32)
                link(dve.tensor_scalar(x, it_i[:, :], k - 7, None, ALU.logical_shift_right))
                link(dve.tensor_scalar(y, it_i[:, :], k - 6, None, ALU.logical_shift_right))
                link(dve.tensor_tensor(x, x, y, ALU.bitwise_xor))
                link(dve.tensor_scalar(y, x, 1, None, ALU.bitwise_and))
                link(dve.tensor_scalar(sgn_l[:, k - 7, :], y, -2.0, 1.0, ALU.mult, ALU.add))

            dve.wait_ge(setup_mm, 1)
            dve.wait_ge(w_in, 64)
            dve.tensor_copy(w1t[:, 0:F], psum[6][:, 0:F])
            dve.tensor_scalar(b1r[:, :], zf[:, :], b1s[:, 0:1], None, ALU.add)
            link(dve.tensor_copy(w1t[:, F:2 * F], psum[6][:, 0:F]))
            dve.sem_inc(const, 1)
            dve.wait_ge(setup_mm, 3)
            dve.tensor_copy(w12[0:F, 0:F], psum[5][0:F, 0:F])
            dve.tensor_copy(w12[F:2 * F, F:2 * F], psum[5][F:2 * F, 0:F])
            link(dve.tensor_copy(c12[:, :], psum[4][:, 0:F]))

            dve.wait_ge(req_in, 16)
            reqf, reqn = k_a[:, 0:RT], k_a[:, RT:2 * RT]
            link(dve.tensor_copy(reqf, req[:, :]))
            link(dve.tensor_scalar(reqn, reqf, 0.0, float(NODES), ALU.is_lt, ALU.mult))
            link(dve.tensor_tensor(reqf, reqf, reqn, ALU.add))
            link(dve.tensor_scalar(req[:, :], reqf, 0.0, float(NODES - 1), ALU.max, ALU.min))

            dve.wait_ge(edge_in, 32)
            low = k_a[0:EP, 0:EC].bitcast(I32)
            link(dve.tensor_scalar(low, dst_raw, P - 1, None, ALU.bitwise_and))
            link(dve.tensor_copy(dlo, low))
            link(dve.tensor_scalar(low, dst_raw, 7, None, ALU.logical_shift_right))
            link(dve.tensor_copy(dhi, low))
            with dve.Fori(0, HB) as i:
                for h in range(2):
                    lane = oh[0:EP, h, 0:P * HT].rearrange("p (j t) -> p j t", t=HT)
                    blk = oh[0:EP, h, P * HT:].rearrange("p (j t) -> p j t", t=HT)
                    dve.wait_ge(hist_mm, i * 2 + (h + 1))
                    for o, d, n in ((lane, dlo, P), (blk, dhi, BLOCKS)):
                        dve.tensor_tensor(o, iorep[0:EP, 0:n, :],
                                          d[:, bass.ds(i * TG + h * HT, HT)].unsqueeze(1).to_broadcast([EP, n, HT]),
                                          ALU.is_equal).then_inc(hist_oh, 1)

            dve.wait_ge(hist_mm, 2 + 2 * HB + 1)
            link(dve.tensor_scalar(deg[:, 0:BLOCKS], psum[7][:, 0:BLOCKS], 1.0, None, ALU.add))
            dve.sem_inc(deg_ready, 1)
            dve.wait_ge(root, 1)
            link(dve.reciprocal(dinv[:, :], nwt[:, :]))
            link(dve.tensor_tensor(nwt[:, :], dinv[:, :], dinv[:, :], ALU.mult))
            link(dve.tensor_tensor(nwt[:, :], nwt[:, :], deg[:, :], ALU.mult))
            link(dve.tensor_scalar(nwt[:, :], nwt[:, :], -0.5, 1.5, ALU.mult, ALU.add))
            link(dve.tensor_tensor(dinv[:, :], dinv[:, :], nwt[:, :], ALU.mult))

            dve.wait_ge(emb_in, 32)
            link(dve.tensor_tensor(acc3, acc3, dinv[:, :].unsqueeze(2).to_broadcast([P, PADB, F]), ALU.mult))
            dve.sem_inc(scaled, 1)

            up = k_a[0:EP, 0:EC].bitcast(I32)
            link(dve.tensor_scalar(up, dst_raw, float(OFF * P), None, ALU.add))
            link(dve.tensor_scalar(dst_raw, up, KSHIFT, None, ALU.logical_shift_left))
            link(dve.tensor_tensor(k_b[0:EP, :].bitcast(I32).rearrange("p (c j) -> p c j", j=COLS)[:, :, 0:CE],
                                   dst_raw.rearrange("p (c j) -> p c j", j=CE),
                                   src_raw.rearrange("p (c j) -> p c j", j=CE), ALU.bitwise_or))

            def signed(src, dst, k):
                a, b = (x[:, :].rearrange("p (g j) -> p g j", j=P) for x in (src, dst))
                dve.tensor_tensor(b, a, sgn_t[:, k:k + 1, :].to_broadcast([P, ALL // P, P]), ALU.mult).then_inc(k_stage, 1)

            def exchange(src, dst, stride):
                a, b = (x[:, :].rearrange("p (g t s) -> p g t s", t=2, s=stride) for x in (src, dst))
                dve.tensor_tensor(b[:, :, 0, :], a[:, :, 0, :], a[:, :, 1, :], ALU.min).then_inc(k_stage, 1)
                dve.tensor_tensor(b[:, :, 1, :], a[:, :, 0, :], a[:, :, 1, :], ALU.max).then_inc(k_stage, 1)

            for what, k, src, dst, before in steps:
                if before:
                    dve.wait_ge(k_stage, before)
                if what == "sign":
                    signed(src, dst, k)
                elif what == "exchange":
                    exchange(src, dst, k)
                elif what == "from_l":
                    for c in range(CHUNKS):
                        dve.wait_ge(tr_l, (k - 8) * CHUNKS + c + 1)
                        dve.tensor_tensor(dst[:, c * COLS:(c + 1) * COLS], psum[c][:, 0:COLS],
                                          sgn_l[:, k - 8, :], ALU.mult).then_inc(ev_l, 1)
                    dve.wait_ge(ev_l, (k - 7) * CHUNKS)
                elif what == "from_t":
                    dve.wait_ge(ev_t, (k - 7) * CHUNKS)

            rows = TILES // CHUNKS
            for c in range(CHUNKS):
                dve.wait_ge(tr_l, len(phases) * CHUNKS + c + 1)
                link(dve.tensor_copy(skey.bitcast(F32).rearrange("p (r c) -> p r c", c=CHUNKS)[:, :, c], psum[c][:, 0:rows]))
            link(dve.tensor_scalar(sidx[:, :], skey, (1 << KSHIFT) - 1, None, ALU.bitwise_and))
            link(dve.tensor_scalar(sdst, skey, KSHIFT, None, ALU.logical_shift_right))
            tmp = k_a[:, 0:TILES].bitcast(I32)
            link(dve.tensor_scalar(tmp, skey, KSHIFT + 7, None, ALU.logical_shift_right))
            link(dve.tensor_scalar(sblk, tmp, float(BLOCKS - 1 + OFF), None, ALU.min))
            dve.sem_inc(prep, 1)
            for c in range(CHUNKS):
                cut = slice(c * rows, (c + 1) * rows)
                dve.wait_ge(bc, c + 1)
                dve.tensor_scalar(blo[0:1, cut], psum[c][0:1, 0:rows], float(-OFF), None, ALU.add)
                dve.scalar_tensor_tensor(out=rel[:, cut], in0=psum[c][:, 0:rows], scalar=float(-P), in1=sdst[:, cut],
                                         op0=ALU.mult, op1=ALU.add).then_inc(prep, 1)
            dve.wait_ge(prep, 1 + CHUNKS)
            for c in range(CHUNKS):
                cut = slice(c * rows, (c + 1) * rows)
                dve.wait_ge(bc, CHUNKS + c + 1)
                link(dve.scalar_tensor_tensor(out=span[0:1, cut], in0=psum[c][0:1, 0:rows], scalar=float(-OFF),
                                              in1=blo[0:1, cut], op0=ALU.add, op1=ALU.subtract))
            link(dve.tensor_reduce(gspan[0:1, :], span[0:1, :].rearrange("p (g t) -> p g t", t=TG), AX.X, ALU.max))
            dve.sem_inc(sorted_ready, 1)

            for layer in range(2):
                base = layer * GROUPS
                with dve.Fori(0, GROUPS) as i:
                    most = dve.value_load(gspan[0:1, bass.ds(i, 1)], min_val=0, max_val=BLOCKS)
                    with dve.If(most >= W):
                        dve.wait_ge(added, (i + base) * TG + FREE_PS)
                        dve.sem_inc(held, 1)
                        with dve.Fori(0, TG) as u:
                            s = dve.value_load(span[0:1, bass.ds(i * TG + u, 1)], min_val=0, max_val=BLOCKS)
                            with dve.If(s >= W):
                                first = dve.value_load(blo[0:1, bass.ds(i * TG + u, 1)], min_val=0, max_val=BLOCKS - 1)
                                chain.add()
                                dve.tensor_scalar(xdst[:, :], skey[:, bass.ds(i * TG + u, 1)], KSHIFT, None,
                                                  ALU.logical_shift_right).then_inc(x_chain, 1)
                                dve.wait_ge(x_chain, chain.value())
                                chain.add()
                                dve.tensor_copy(xdsf[:, :], xdst[:, :]).then_inc(x_chain, 1)
                                dve.wait_ge(x_chain, chain.value())
                                dve.sem_inc(held, 1)
                                with dve.Fori(W, s + 1) as j:
                                    visits.add()
                                    dve.reg_add(blk_reg, first, j)
                                    at_blk = dve.snap(blk_reg, min_val=0, max_val=BLOCKS - 1)
                                    dve.tensor_scalar(xoh[:, :], colf[:, :], xblk[:, bass.ds(at_blk, 1)], xdsf[:, 0:1],
                                                      ALU.add, ALU.is_equal).then_inc(x_oh, 1)
                                    dve.wait_ge(x_mm, visits.value())
                                    rows_of = acc[:, bass.ds(at_blk * F, F)]
                                    chain.add()
                                    dve.tensor_tensor(rows_of, psum[4][:, 0:F], rows_of, ALU.add).then_inc(x_chain, 1)
                                    dve.wait_ge(x_chain, chain.value())
                                dve.nop()
                            dve.nop()
                        dve.nop()
                    for u in range(TG):
                        if u % HT == 0:
                            dve.tensor_tensor(ohw, iorep[:, :, :],
                                              rel[:, bass.ds(i * TG + u, HT)].unsqueeze(1).to_broadcast([P, W * P, HT]),
                                              ALU.is_equal).then_inc(oh_ready, 1)
                            firsts = load_row(dve, blo[0:1, bass.ds(i * TG + u, HT)], BLOCKS - 1)
                        first = firsts[u % HT]
                        dve.wait_ge(mm_done, (i + base) * TG + (u + 1 + FREE_MM))
                        dve.wait_ge(added, (i + base) * TG + (u + FREE_PS))
                        window = acc[:, bass.ds(first * F, W * F)]
                        dve.tensor_tensor(window, psum[u % NPS][:, 0:W * F], window, ALU.add).then_inc(added, 1)

                if layer == 0:
                    dve.wait_ge(added, GROUPS * TG + FREE_PS)
                    dve.sem_inc(node_st, 1)

                    def node_rows(g, s, i):
                        a3 = acc[:, bass.ds(g * (BB * F), BB * F)].rearrange("p (b f) -> p b f", f=F)
                        d3 = dinv[:, bass.ds(g * BB, BB)].unsqueeze(2).to_broadcast([P, BB, F])
                        wait_if(dve, node_mm, g)
                        dve.tensor_tensor(stage[:, :].rearrange("p (b f) -> p b f", f=F), a3, d3, ALU.mult).then_inc(node_st, 1)
                        dve.wait_ge(node_mm, g + 1)
                        dve.tensor_tensor(tnode[:, :].rearrange("p (b f) -> p b f", f=F),
                                          psum[6][:, :].rearrange("p (b f) -> p b f", f=F),
                                          c12[:, :].unsqueeze(1).to_broadcast([P, BB, F]), ALU.add).then_inc(node_st, 1)
                        dve.wait_ge(node_st, g * 3 + 3)
                        dve.tensor_tensor(a3, tnode[:, :].rearrange("p (b f) -> p b f", f=F), d3, ALU.mult).then_inc(node_st, 1)
                    batches(dve, node_rows)

            dve.wait_ge(added, 2 * GROUPS * TG + FREE_PS)
            link(dve.tensor_tensor(acc3, acc3, dinv[:, :].unsqueeze(2).to_broadcast([P, PADB, F]), ALU.mult))
            link(dve.tensor_tensor(acc3, acc3, b2r[:, :].unsqueeze(1).to_broadcast([P, PADB, F]), ALU.add))
            dve.sem_inc(rows_ready, 1)


_INS = ["r_input", "L0_rec_emb", "L0_rec_W1", "L0_rec_b1", "L0_rec_W2", "L0_rec_b2", "L0_rec_edge_index"]


def kernel(**inputs):
    import numpy as np
    import concourse.bacc as bacc
    from concourse.bass_utils import run_bass_kernel_spmd

    nc = bacc.Bacc("TRN2", target_bir_lowering=False, num_devices=1)
    arrays, args = {}, []
    for name in _INS:
        a = np.ascontiguousarray(inputs[name])
        arrays["in_" + name] = a
        args.append(nc.dram_tensor("in_" + name, a.shape, mybir.dt.from_np(a.dtype), kind="ExternalInput").ap())
    out = nc.dram_tensor("out", (BATCH, SEQ, F), F32, kind="ExternalOutput").ap()
    gcn_program(nc, *args, out)
    r = run_bass_kernel_spmd(nc, [arrays], core_ids=[0])
    return r.results[0]["out"]
```

```python
from contextlib import ExitStack

import concourse.bass as bass
from concourse import mybir

ALU = mybir.AluOpType
ACT = mybir.ActivationFunctionType
AX = mybir.AxisListType
F32 = mybir.dt.float32
BF16 = mybir.dt.bfloat16
I32 = mybir.dt.int32
I16 = mybir.dt.int16

P = 128
NODES, F, HID, EDGES = 18750, 64, 128, 300000
BATCH, SEQ = 512, 200
REQS = BATCH * SEQ
RT = REQS // P
LAST = NODES - 1
OG = 20
QG = 7
ROUND = OG * QG
RCOLS = -(-RT // ROUND) * ROUND
FILL = 25

BLOCKS = -(-NODES // P)
BB = 8
NBATCH = 19
PADB = BB * NBATCH
FULLB = NODES // P
TAIL = NODES - FULLB * P
PARTS = 3
ROW = PARTS * F

CHUNKS, SB = 5, 16
COLS = (1 << SB) // P
ALL = CHUNKS * COLS
EP = 125
EC = EDGES // EP
CE = EC // CHUNKS
OFF = 2
KSHIFT = 15
PADKEY = float(2 ** 127)
TG = 20
HT = TG // 2
GROUPS = -(-(-(-EC * EP // CHUNKS // P)) * CHUNKS // TG)
TILES = GROUPS * TG
W = 2
HB = EC // TG


def gcn_program(nc, r_input, emb, w1, b1, w2, b2, edges, out):
    table = nc.dram_tensor("table", (PADB * P, ROW), BF16, kind="Internal").ap()
    marks = nc.dram_tensor("marks", (2 * P, P), BF16, kind="Internal").ap()
    last = nc.dram_tensor("last", (1, F), F32, kind="Internal").ap()
    nodes = nc.dram_tensor("nodes", (NODES, F), F32, kind="Internal").ap()

    ctx = ExitStack()
    with ctx:
        def sb(name, shape, dt):
            return ctx.enter_context(nc.sbuf_tensor(name, shape, dt))

        def sem(name):
            return ctx.enter_context(nc.semaphore(name))

        acc = sb("acc", [P, PADB * F], F32)
        acc3 = acc[:, :].rearrange("p (b f) -> p b f", f=F)
        raw = sb("raw", [P, 3 * EC], I32)
        dst_raw, src_raw = raw[0:EP, 0:EC], raw[0:EP, EC:2 * EC]
        dlo = raw[0:EP, 2 * EC:2 * EC + EC // 2].bitcast(BF16)
        dhi = raw[0:EP, 2 * EC + EC // 2:3 * EC].bitcast(BF16)
        skey = raw[:, 0:TILES]
        sidx = sb("sidx", [P, TILES], I32)
        sdst = raw[:, EC:EC + TILES]
        rel = raw[:, 2 * EC:2 * EC + TILES // 2].bitcast(BF16)
        sblk = raw[:, 2 * EC + EC // 2:2 * EC + EC // 2 + TILES // 2].bitcast(BF16)
        work = sb("work", [P, PADB * P // 2], F32)
        wanted = work[:, :].bitcast(BF16)
        cut = [0]

        def carve(n):
            cut[0] += n
            return work[:, cut[0] - n:cut[0]]

        k_a, k_b = carve(ALL), carve(ALL)
        stage, zt, tnode = carve(BB * F), carve(BB * F), carve(BB * F)
        res = carve(2 * BB * F).rearrange("p (n f) -> p n f", n=2)
        tab = carve(BB * ROW).bitcast(BF16).rearrange("p (s b f) -> p s b f", s=2, f=ROW)
        sgn_t = sb("sgn_t", [P, 7, P], BF16)
        sgn_l = sb("sgn_l", [P, SB - 7, COLS], BF16)
        io_r = sb("io_r", [P, RT], I32)
        it_i = io_r[:, 0:COLS]
        it_x = sb("it_x", [P, P], I32)
        it_y = sb("it_y", [P, 1], I32)
        iorep = sb("iorep", [P, W * P, HT], BF16)
        oh = sb("oh", [P, 2, (P + BLOCKS) * HT], BF16)
        ohw = oh[:, 0, 0:W * P * HT].rearrange("p (j t) -> p j t", t=HT)
        ring = sb("ring", [P, TG, ROW], BF16)
        gidx = sb("gidx", [P, TG], I32)
        keep = sb("keep", [P, TILES], F32)
        junk = sb("junk", [P, W * P], BF16)
        valid = sb("valid", [1, TILES], F32)
        vgrp = sb("vgrp", [1, GROUPS], F32)
        ngrp = sb("ngrp", [1, 1], I32)
        mask = sb("mask", [P, 2 * P], F32)
        maskt = sb("maskt", [P, 2, P], BF16)
        rlo, rhi = (keep[:, n * (RT // 2):(n + 1) * (RT // 2)].bitcast(BF16) for n in range(2))
        blo = sb("blo", [1, TILES], I16)
        span = sb("span", [1, TILES], I16)
        gspan = sb("gspan", [1, GROUPS], I16)
        dinv = sb("dinv", [P, PADB], F32)
        deg = sb("deg", [P, PADB], F32)
        nwt = sb("nwt", [P, PADB], F32)
        colf = sb("colf", [P, P], F32)
        rowf = sb("rowf", [P, 1], F32)
        ident = sb("ident", [P, P], F32)
        sel = sb("sel", [P, 2, P], BF16)
        zero = sb("zero", [P, BLOCKS], BF16)
        zf = sb("zf", [P, P], F32)
        w1s = sb("w1s", [F, HID], F32)
        w1t = sb("w1t", [HID, P], F32)
        w2s = sb("w2s", [HID, F], F32)
        b1s = sb("b1s", [HID, 1], F32)
        b1r = sb("b1r", [HID, P], F32)
        b2r = sb("b2r", [P, F], F32)
        w12 = sb("w12", [P, P], F32)
        c12 = sb("c12", [P, F], F32)
        req = sb("req", [P, RT], I32)
        oidx = sb("oidx", [P, 2, ROUND], I32)
        reqkey = sb("reqkey", [P, RT], F32)
        top8 = sb("top8", [P, 8], F32)
        comp = sb("comp", [P, GROUPS * 8], F32)
        ccol = sb("ccol", [P, 2, RCOLS], I32)
        cnt = sb("cnt", [P, 1], F32)
        nreq = sb("nreq", [1, 2], I32)
        nrf = sb("nrf", [1, 8], F32)
        pbase = sb("pbase", [P, 1], F32)
        lrow = sb("lrow", [P, F], F32)
        fill = k_a[:, 0:FILL * F]
        xblk = sb("xblk", [P, PADB], F32)
        xdst = sb("xdst", [P, 1], I32)
        xdsf = sb("xdsf", [P, 1], F32)
        xoh = sb("xoh", [P, P], BF16)

        psum = [ctx.enter_context(nc.psum_tensor(f"ps{i}", [P, 512], F32)) for i in range(8)]

        marks_out = sem("marks_out")
        wanted_in = sem("wanted_in")
        emb_in = sem("emb_in")
        edge_in = sem("edge_in")
        w_in = sem("w_in")
        req_in = sem("req_in")
        iotas = sem("iotas")
        const = sem("const")
        hist_oh = sem("hist_oh")
        hist_mm = sem("hist_mm")
        step = sem("step")
        deg_ready = sem("deg_ready")
        root = sem("root")
        scaled = sem("scaled")
        part_act = sem("part_act")
        part_pool = sem("part_pool")
        tab_out = [sem(f"tab_out{s}") for s in range(2)]
        stage_done = sem("stage_done")
        k_stage = sem("k_stage")
        tr_l = sem("tr_l")
        tr_t = sem("tr_t")
        ev_l = sem("ev_l")
        ev_t = sem("ev_t")
        prep = sem("prep")
        bc = sem("bc")
        sorted_ready = sem("sorted_ready")
        idx_ready = sem("idx_ready")
        gathered = [sem(f"gathered{u}") for u in range(TG)]
        oh_ready = sem("oh_ready")
        mm_done = sem("mm_done")
        added = sem("added")
        flagged = sem("flagged")
        x_oh = sem("x_oh")
        x_mm = sem("x_mm")
        x_chain = sem("x_chain")
        held = sem("held")
        setup_mm = sem("setup_mm")
        node_st = sem("node_st")
        node_tr = sem("node_tr")
        node_zt = sem("node_zt")
        node_mm = sem("node_mm")
        rows_ready = sem("rows_ready")
        nodes_out = sem("nodes_out")
        taken = sem("taken")
        comp_done = sem("comp_done")
        counts = sem("counts")
        counts_in = sem("counts_in")
        count_tr = sem("count_tr")
        last_out = sem("last_out")
        last_in = sem("last_in")
        fill_ready = sem("fill_ready")
        filled = sem("filled")
        out_idx = sem("out_idx")
        round_done = sem("round_done")
        got = [sem(f"got{q}") for q in range(QG)]
        put = [sem(f"put{q}") for q in range(QG)]

        block = ctx.enter_context(nc.Block())

        def batches(eng, body):
            for s in range(2):
                body(s, s, 0)
            with eng.Fori(1, NBATCH // 2) as i:
                for s in range(2):
                    body(i * 2 + s, s, i)
            body(NBATCH - 1, 0, NBATCH // 2)

        REQ_MM = RT // HT + 1
        FREE_MM, FREE_PS = TG, 4
        NPS = 4
        PIECES = [(0, 37), (37, 74), (74, 110), (110, FULLB)]

        phases = range(8, SB + 1)
        steps = [("sign", 0, k_b, k_a, 0)]
        turns = []
        turned = []
        done, cur, other = 1, k_a, k_b
        for k in range(1, SB + 1):
            if 1 < k < 8:
                steps.append(("sign", k - 1, cur, other, done))
                done, cur, other = done + 1, other, cur
            for bit in range(k - 1, -1, -1):
                fresh = k >= 8 and bit in (k - 1, 6)
                if fresh:
                    turns.append((done, cur))
                    cur, other = other, cur
                    steps.append(("from_l" if bit == k - 1 else "from_t", k, None, cur, 0))
                    if bit == 6:
                        turned.append(cur)
                stride = 1 << (bit - 7 if bit >= 7 else bit)
                steps.append(("exchange", stride, cur, other, 0 if fresh else done))
                done, cur, other = done + 2, other, cur
        turns.append((done, cur))
        SORT_STEPS = done
        TO_L, TO_T = (len(turns) + 1) // 2 * CHUNKS, len(turns) // 2 * CHUNKS

        def turn(pe, src, signal):
            for c in range(CHUNKS):
                for q in range(COLS // P):
                    mm = pe.transpose(psum[c][:, q * P:(q + 1) * P],
                                      src[:, c * COLS + q * P:c * COLS + (q + 1) * P], ident[:, :])
                mm.then_inc(signal, 1)

        def load_row(eng, ap, most):
            return nc.values_load_multi_w_load_instructions(
                ap, engines=[eng.engine], min_val=0, max_val=most,
                skip_runtime_bounds_check_because="the rows hold clamped block numbers")[1]

        def wait_if(eng, signal, value):
            if not (isinstance(value, int) and value == 0):
                eng.wait_ge(signal, value)

        def peeled(eng, n, body):
            body(0)
            with eng.Fori(1, n) as i:
                body(i)

        def groups_of(eng, layer):
            return eng.value_load(ngrp[0:1, 0:1], min_val=1, max_val=GROUPS) if layer else GROUPS

        class Count:

            def __init__(self, eng, name):
                self.eng, self.reg = eng, eng.alloc_register(name)
                eng.reg_mov(self.reg, 0)

            def add(self):
                self.eng.reg_add(self.reg, self.reg, 1)

            def value(self):
                return self.eng.snap(self.reg, min_val=0, max_val=1 << 24)

        @block.sync
        def _(sp):
            sp.dma_start(dst_raw, edges[1].rearrange("(p j) -> p j", p=EP)).then_inc(edge_in, 16)
            sp.dma_start(src_raw, edges[0].rearrange("(p j) -> p j", p=EP)).then_inc(edge_in, 16)
            sp.dma_start(w1s[:, :], w1).then_inc(w_in, 16)
            sp.dma_start(w2s[:, :], w2).then_inc(w_in, 16)
            sp.dma_start(b1s[:, :], b1.rearrange("(h a) -> h a", a=1)).then_inc(w_in, 16)
            sp.dma_start(b2r[:, :], b2.rearrange("(a f) -> a f", a=1).to_broadcast([P, F])).then_inc(w_in, 16)
            sp.dma_start(req[:, :], r_input.rearrange("a b -> (a b)").rearrange("(p t) -> p t", p=P)).then_inc(req_in, 16)
            sp.wait_ge(const, 1)
            sp.dma_start(acc3[:, 0:FULLB, :], emb[0:FULLB * P, :].rearrange("(b p) f -> p b f", p=P)).then_inc(emb_in, 16)
            sp.dma_start(acc3[0:TAIL, FULLB, :], emb[FULLB * P:NODES, :]).then_inc(emb_in, 16)

            sp.wait_ge(const, 5)
            sp.dma_start(marks.rearrange("(n p) j -> p n j", p=P), maskt[:, :, :]).then_inc(marks_out, 16)

            for layer in range(2):
                def store(g, s, i):
                    sp.wait_ge(part_act, PARTS * (g + 1 + layer * NBATCH))
                    rows = table[bass.ds(g * (BB * P), BB * P), :].rearrange("(b p) f -> p b f", p=P)
                    sp.dma_start(rows, tab[:, s]).then_inc(tab_out[s], 16)
                batches(sp, store)
                if layer == 0:
                    sp.wait_ge(marks_out, 16)
                    sp.wait_ge(sorted_ready, 1)
                    sp.wait_ge(tab_out[0], 16 * (NBATCH // 2 + 1))
                    sp.wait_ge(tab_out[1], 16 * (NBATCH // 2))
                    sp.dma_start(wanted, marks.rearrange("(a n) j -> a (n j)", a=1)[:, 0:PADB * P].to_broadcast([P, PADB * P])).then_inc(wanted_in, 16)

            sp.wait_ge(rows_ready, 1)
            sp.dma_start(last, acc3[(LAST % P):(LAST % P) + 1, LAST // P, :]).then_inc(last_out, 16)
            sp.wait_ge(last_out, 16)
            sp.dma_start(lrow[:, :], last.to_broadcast([P, F])).then_inc(last_in, 16)
            for n, (blk0, blk1) in enumerate(PIECES):
                sp.wait_ge(rows_ready, n + 2)
                sp.dma_start(nodes[blk0 * P:blk1 * P, :].rearrange("(b p) f -> p b f", p=P), acc3[:, blk0:blk1, :]).then_inc(nodes_out, 16)
            sp.dma_start(nodes[FULLB * P:NODES, :], acc3[0:TAIL, FULLB, :]).then_inc(nodes_out, 16)

            rows = out.rearrange("a b f -> (a b) f").rearrange("(p r t) f -> p r (t f)", p=P, t=FILL)
            sp.wait_ge(fill_ready, 1)
            sp.dma_start(rows, fill.unsqueeze(1).to_broadcast([P, RT // FILL, FILL * F])).then_inc(filled, 16)
            sp.wait_ge(filled, 16)

        @block.gpsimd
        def _(pool):
            pool.iota(io_r[:, :], pattern=[[1, RT]], base=0, channel_multiplier=0).then_inc(iotas, 1)
            pool.iota(it_x[:, 0:P], pattern=[[1, P]], base=0, channel_multiplier=P).then_inc(iotas, 1)
            pool.iota(it_y[:, 0:1], pattern=[[1, 1]], base=0, channel_multiplier=1).then_inc(iotas, 1)
            pool.iota(iorep[:, :, :], pattern=[[1, W * P], [0, HT]], base=0, channel_multiplier=0,
                      allow_small_or_imprecise_dtypes=True).then_inc(iotas, 1)

            for layer in range(2):
                def rest(g, s, i):
                    b = g + layer * NBATCH
                    x = acc[:, bass.ds(g * (BB * F), BB * F)].rearrange("p (b f) -> p b f", f=F)
                    r = [res[:, n, :].rearrange("p (b f) -> p b f", f=F) for n in range(2)]
                    pool.wait_ge(part_act, b * PARTS + 1)
                    pool.tensor_tensor(r[0], x, tab[:, s, :, 0:F], ALU.subtract).then_inc(part_pool, 1)
                    pool.wait_ge(part_pool, b * 2 + 1)
                    pool.wait_ge(part_act, b * PARTS + 2)
                    pool.tensor_tensor(r[1], r[0], tab[:, s, :, F:2 * F], ALU.subtract).then_inc(part_pool, 1)
                batches(pool, rest)

                pool.wait_ge(tab_out[0], 16 * (NBATCH // 2 + 1) * (layer + 1))
                pool.wait_ge(tab_out[1], 16 * (NBATCH // 2) * (layer + 1))
                if layer:
                    pool.wait_ge(sorted_ready, layer + 1)
                with pool.Fori(0, groups_of(pool, layer)) as i:
                    for u in range(TG):
                        if u % HT == 0:
                            pool.wait_ge(idx_ready, (i + layer * GROUPS) * 2 + (u // HT + 1))
                            pool.sem_inc(held, 1)
                        pool.indirect_dma_start(
                            out=ring[:, u, :], out_offset=None, in_=table,
                            in_offset=bass.IndirectOffsetOnAxis(ap=gidx[:, u:u + 1], axis=0)).then_inc(gathered[u], 16)

            result = out.rearrange("a b f -> (a b) f")
            pool.wait_ge(counts, 1)
            most = pool.value_load(nreq[0:1, 0:1], min_val=0, max_val=RT)
            rounds = pool.value_load(nreq[0:1, 1:2], min_val=1, max_val=RCOLS // ROUND)
            pool.sem_inc(round_done, 1)
            pool.wait_ge(nodes_out, 16 * (len(PIECES) + 1))
            with pool.Fori(0, rounds) as r:
                pool.wait_ge(out_idx, r + 1)
                pool.sem_inc(held, 1)
                for q in range(QG):
                    with pool.If(most > r * ROUND + q * OG):
                        for t in range(q * OG, (q + 1) * OG):
                            pool.indirect_dma_start(
                                out=acc[:, t * F:(t + 1) * F], out_offset=None, in_=nodes,
                                in_offset=bass.IndirectOffsetOnAxis(ap=oidx[:, 0, t:t + 1], axis=0)).then_inc(got[q], 16)
                pool.wait_ge(filled, 16)
                for q in range(QG):
                    with pool.If(most > r * ROUND + q * OG):
                        pool.wait_ge(got[q], (r + 1) * (16 * OG))
                        pool.sem_inc(held, 1)
                        for t in range(q * OG, (q + 1) * OG):
                            pool.indirect_dma_start(
                                out=result, out_offset=bass.IndirectOffsetOnAxis(ap=oidx[:, 1, t:t + 1], axis=0),
                                in_=acc[:, t * F:(t + 1) * F], in_offset=None,
                                bounds_check=REQS - 1, oob_is_err=False).then_inc(put[q], 16)
                for q in range(QG):
                    with pool.If(most > r * ROUND + q * OG):
                        pool.wait_ge(put[q], (r + 1) * (16 * OG))
                        pool.sem_inc(held, 1)
                pool.sem_inc(round_done, 1)

        @block.scalar
        def _(act):
            act.sem_inc(comp_done, 1)
            act.wait_ge(deg_ready, 1)
            act.activation(nwt[:, :], deg[:, :], ACT.Sqrt).then_inc(root, 1)

            for layer in range(2):
                def parts(g, s, i):
                    b = g + layer * NBATCH
                    x = acc[:, bass.ds(g * (BB * F), BB * F)].rearrange("p (b f) -> p b f", f=F)
                    r = [res[:, n, :].rearrange("p (b f) -> p b f", f=F) for n in range(2)]
                    if layer == 0:
                        act.wait_ge(scaled, 1)
                    else:
                        act.wait_ge(node_st, 1 + g * 3 + 3)
                    if layer == 0:
                        wait_if(act, tab_out[s], i * 16)
                    else:
                        act.wait_ge(tab_out[s], (i + (NBATCH // 2 + 1 - s)) * 16)
                    act.activation(tab[:, s, :, 0:F], x, ACT.Copy).then_inc(part_act, 1)
                    act.wait_ge(part_pool, b * 2 + 1)
                    act.activation(tab[:, s, :, F:2 * F], r[0], ACT.Copy).then_inc(part_act, 1)
                    act.wait_ge(part_pool, b * 2 + 2)
                    act.activation(tab[:, s, :, 2 * F:3 * F], r[1], ACT.Copy).then_inc(part_act, 1)

                def nodes_t(g):
                    act.wait_ge(node_tr, g + 1)
                    act.activation(zt[:, :], psum[5][:, :], ACT.Copy).then_inc(node_zt, 1)
                    parts(g, g % 2, g // 2)

                if layer == 0:
                    batches(act, parts)
                else:
                    nodes_t(0)
                for n, dst in enumerate(turned):
                    for c in range(CHUNKS):
                        act.wait_ge(tr_t, (layer * len(turned) + n) * CHUNKS + c + 1)
                        act.activation(dst[:, c * COLS:(c + 1) * COLS], psum[c][:, 0:COLS], ACT.Copy).then_inc(ev_t, 1)
                    if layer:
                        nodes_t(2 * n + 1)
                        nodes_t(2 * n + 2)

                act.wait_ge(sorted_ready, layer + 1)
                with act.Fori(0, groups_of(act, layer)) as i:
                    for h in range(2):
                        act.wait_ge(mm_done, (i + layer * GROUPS) * TG + (h + 1) * HT)
                        act.copy(gidx[:, h * HT:(h + 1) * HT],
                                 sidx[:, bass.ds(i * TG + h * HT, HT)]).then_inc(idx_ready, 1)
                    if layer == 0:
                        act.wait_ge(taken, i * 2 + 2)
                        act.copy(comp[:, bass.ds(i * 8, 8)], top8[:, :]).then_inc(comp_done, 1)

            act.wait_ge(counts, 1)
            rounds = act.value_load(nreq[0:1, 1:2], min_val=1, max_val=RCOLS // ROUND)
            with act.Fori(0, rounds) as r:
                act.wait_ge(round_done, r + 1)
                act.copy(oidx[:, :, :], ccol[:, :, bass.ds(r * ROUND, ROUND)]).then_inc(out_idx, 1)

        @block.tensor
        def _(pe):
            visits = Count(pe, "pe_visits")

            def sort_turns(rnd, between):
                for n, (ready, src) in enumerate(turns):
                    pe.wait_ge(k_stage, rnd * SORT_STEPS + ready)
                    if n % 2:
                        pe.wait_ge(ev_l, rnd * (TO_L - CHUNKS) + (n + 1) // 2 * CHUNKS)
                    elif n + rnd:
                        pe.wait_ge(ev_t, rnd * TO_T + n // 2 * CHUNKS)
                    turn(pe, src, tr_t if n % 2 else tr_l)
                    if between:
                        between(n)

            def tile_blocks(rnd):
                n = TILES // CHUNKS
                for e in range(2):
                    pe.wait_ge(prep, rnd * (1 + CHUNKS) + 1 + CHUNKS * e)
                    for c in range(CHUNKS):
                        pe.matmul(psum[c][:, 0:n], sel[:, e, :], sblk[:, c * n:(c + 1) * n],
                                  start=True, stop=True).then_inc(bc, 1)

            pe.sem_inc(mm_done, FREE_MM)
            pe.sem_inc(hist_mm, 2)
            pe.wait_ge(const, 2)
            pe.wait_ge(w_in, 64)
            pe.transpose(psum[6][:, 0:F], w1s[:, :], ident[0:F, 0:F]).then_inc(setup_mm, 1)
            pe.wait_ge(const, 3)
            pe.matmul(psum[5][:, 0:F], w1t[:, :], w2s[:, :], start=True, stop=True).then_inc(setup_mm, 1)
            pe.matmul(psum[4][:, 0:F], b1r[:, :], w2s[:, :], start=True, stop=True).then_inc(setup_mm, 1)

            pe.matmul(psum[7][:, 0:BLOCKS], sel[:, 0, :], zero[:, :], start=True, stop=False)
            with pe.Fori(0, RT // TG) as i:
                for h in range(2):
                    lane = oh[:, h, 0:P * HT].rearrange("p (j t) -> p j t", t=HT)
                    blk = oh[:, h, P * HT:].rearrange("p (j t) -> p j t", t=HT)
                    pe.wait_ge(hist_oh, i * 4 + (2 * h + 2))
                    for t in range(HT):
                        mm = pe.matmul(psum[7][:, 0:BLOCKS], lane[:, :, t], blk[:, :, t], start=False, stop=False)
                    mm.then_inc(hist_mm, 1)
            pe.matmul(psum[7][:, 0:BLOCKS], sel[:, 0, :], zero[:, :], start=False, stop=True).then_inc(hist_mm, 1)
            pe.wait_ge(const, 4)
            for n in range(2):
                pe.transpose(psum[6][:, n * P:(n + 1) * P], mask[:, n * P:(n + 1) * P], ident[:, :]).then_inc(setup_mm, 1)

            pe.matmul(psum[7][:, 0:BLOCKS], sel[:, 0, :], zero[:, :], start=True, stop=False)
            with pe.Fori(0, HB) as i:
                for h in range(2):
                    lane = oh[0:EP, h, 0:P * HT].rearrange("p (j t) -> p j t", t=HT)
                    blk = oh[0:EP, h, P * HT:].rearrange("p (j t) -> p j t", t=HT)
                    pe.wait_ge(hist_oh, i * 4 + (RT // HT * 2 + 2 * h + 2))
                    for t in range(HT):
                        mm = pe.matmul(psum[7][:, 0:BLOCKS], lane[:, :, t], blk[:, :, t], start=False, stop=False)
                    mm.then_inc(hist_mm, 1)
            pe.matmul(psum[7][:, 0:BLOCKS], sel[:, 0, :], zero[:, :], start=False, stop=True).then_inc(hist_mm, 1)

            sort_turns(0, None)
            tile_blocks(0)

            for layer in range(2):
                pe.wait_ge(sorted_ready, layer + 1)
                with pe.Fori(0, groups_of(pe, layer)) as i:
                    most = pe.value_load(gspan[0:1, bass.ds(i, 1)], min_val=0, max_val=BLOCKS)
                    with pe.If(most >= W):
                        for u in range(TG):
                            pe.wait_ge(gathered[u], (i + (layer * GROUPS + 1)) * 16)
                        pe.sem_inc(held, 1)
                        with pe.Fori(0, TG) as u:
                            s = pe.value_load(span[0:1, bass.ds(i * TG + u, 1)], min_val=0, max_val=BLOCKS)
                            with pe.If(s >= W):
                                with pe.Fori(W, s + 1) as j:
                                    visits.add()
                                    pe.wait_ge(x_oh, visits.value())
                                    for a in range(PARTS):
                                        mm = pe.matmul(psum[4][:, 0:F], xoh[:, :],
                                                       ring[:, :, :].rearrange("p u f -> p (u f)")[:, bass.ds(u * ROW + a * F, F)],
                                                       start=(a == 0), stop=(a == PARTS - 1))
                                    mm.then_inc(x_mm, 1)
                                pe.nop()
                            pe.nop()
                        pe.nop()
                    for u in range(TG):
                        if u % HT == 0:
                            pe.wait_ge(oh_ready, (i + layer * GROUPS) * 2 + (u // HT + 1))
                        pe.wait_ge(gathered[u], (i + (layer * GROUPS + 1)) * 16)
                        pe.wait_ge(added, (i + layer * GROUPS) * TG + (u + 1))
                        for w in range(W):
                            for a in range(PARTS):
                                mm = pe.matmul(psum[u % NPS][:, w * F:(w + 1) * F],
                                               ohw[:, w * P:(w + 1) * P, u % HT], ring[:, u, a * F:(a + 1) * F],
                                               start=(a == 0), stop=(a == PARTS - 1))
                        mm.then_inc(mm_done, 1)
                if layer == 0:
                    def node_rows(g):
                        pe.wait_ge(node_st, g * 3 + 1 + 1)
                        for q in range(BB // 2):
                            mm = pe.transpose(psum[5][:, q * P:(q + 1) * P], stage[:, q * P:(q + 1) * P], ident[:, :])
                        mm.then_inc(node_tr, 1)
                        pe.wait_ge(node_zt, g + 1)
                        for q in range(BB // 2):
                            mm = pe.matmul(psum[6][:, q * P:(q + 1) * P], zt[:, q * P:(q + 1) * P], w12[:, :],
                                           start=True, stop=True)
                        mm.then_inc(node_mm, 1)
                    pe.wait_ge(counts_in, 1)
                    pe.transpose(psum[7][0:1, 0:P], cnt[:, 0:1], ident[:, :]).then_inc(count_tr, 1)
                    sort_turns(1, node_rows)
                    tile_blocks(1)

        @block.vector
        def _(dve):
            visits = Count(dve, "dve_visits")
            chain = Count(dve, "dve_chain")
            blk_reg = dve.alloc_register("dve_block")
            at = [0]

            def link(ins):
                at[0] += 1
                ins.then_inc(step, 1)
                dve.wait_ge(step, at[0])

            def one_hots(n, parts, lanes, blocks, base):
                with dve.Fori(0, n) as i:
                    for h in range(2):
                        lane = oh[0:parts, h, 0:P * HT].rearrange("p (j t) -> p j t", t=HT)
                        blk = oh[0:parts, h, P * HT:].rearrange("p (j t) -> p j t", t=HT)
                        dve.wait_ge(hist_mm, i * 2 + (h + 1 + base))
                        for o, d, m in ((lane, lanes, P), (blk, blocks, BLOCKS)):
                            dve.tensor_tensor(o, iorep[0:parts, 0:m, :],
                                              d[0:parts, bass.ds(i * TG + h * HT, HT)].unsqueeze(1).to_broadcast([parts, m, HT]),
                                              ALU.is_equal).then_inc(hist_oh, 1)

            dve.sem_inc(added, FREE_PS)
            dve.sem_inc(flagged, 1)
            dve.sem_inc(taken, 1)
            link(dve.memset(acc[:, FULLB * F:], 0.0))
            dve.sem_inc(const, 1)

            dve.memset(zero[:, :], 0.0)
            dve.memset(w12[:, :], 0.0)
            dve.memset(zf[:, :], 0.0)
            dve.memset(deg[:, :], 1.0)
            link(dve.memset(k_b[:, :], PADKEY))
            dve.wait_ge(iotas, 4)
            dve.tensor_copy(colf[:, :], it_i[:, 0:P])
            link(dve.tensor_copy(rowf[:, :], it_y[:, 0:1]))
            link(dve.tensor_scalar(ident[:, :], colf[:, :], rowf[:, 0:1], None, ALU.is_equal))
            link(dve.tensor_copy(sel[:, 0, :], ident[:, 0:1].to_broadcast([P, P])))
            link(dve.tensor_copy(sel[:, 1, :], ident[:, P - 1:P].to_broadcast([P, P])))
            link(dve.tensor_scalar(xblk[:, :], it_i[:, 0:PADB], float(P), float(OFF * P), ALU.mult, ALU.add))
            dve.sem_inc(const, 1)
            for k in range(7):
                if k == 0:
                    link(dve.tensor_scalar(k_a[:, 0:P].bitcast(I32), it_x[:, 0:P], 1, 1, ALU.logical_shift_right, ALU.bitwise_and))
                else:
                    link(dve.tensor_scalar(k_a[:, P:2 * P].bitcast(I32), it_x[:, 0:P], k, None, ALU.logical_shift_right))
                    link(dve.tensor_scalar(k_a[:, 0:P].bitcast(I32), it_x[:, 0:P], k + 1, None, ALU.logical_shift_right))
                    link(dve.tensor_tensor(k_a[:, P:2 * P].bitcast(I32), k_a[:, 0:P].bitcast(I32), k_a[:, P:2 * P].bitcast(I32), ALU.bitwise_xor))
                    link(dve.tensor_scalar(k_a[:, 0:P].bitcast(I32), k_a[:, P:2 * P].bitcast(I32), 1, None, ALU.bitwise_and))
                link(dve.tensor_scalar(sgn_t[:, k, :], k_a[:, 0:P].bitcast(I32), -2.0, 1.0, ALU.mult, ALU.add))
            for k in range(7, SB):
                x = k_a[:, 0:COLS].bitcast(I32)
                y = k_a[:, COLS:2 * COLS].bitcast(I32)
                link(dve.tensor_scalar(x, it_i, k - 7, None, ALU.logical_shift_right))
                link(dve.tensor_scalar(y, it_i, k - 6, None, ALU.logical_shift_right))
                link(dve.tensor_tensor(x, x, y, ALU.bitwise_xor))
                link(dve.tensor_scalar(y, x, 1, None, ALU.bitwise_and))
                link(dve.tensor_scalar(sgn_l[:, k - 7, :], y, -2.0, 1.0, ALU.mult, ALU.add))

            dve.wait_ge(setup_mm, 1)
            dve.wait_ge(w_in, 64)
            dve.tensor_copy(w1t[:, 0:F], psum[6][:, 0:F])
            dve.tensor_scalar(b1r[:, :], zf[:, :], b1s[:, 0:1], None, ALU.add)
            link(dve.tensor_copy(w1t[:, F:2 * F], psum[6][:, 0:F]))
            dve.sem_inc(const, 1)
            dve.wait_ge(setup_mm, 3)
            dve.tensor_copy(w12[0:F, 0:F], psum[5][0:F, 0:F])
            dve.tensor_copy(w12[F:2 * F, F:2 * F], psum[5][F:2 * F, 0:F])
            link(dve.tensor_copy(c12[:, :], psum[4][:, 0:F]))

            dve.wait_ge(req_in, 16)
            reqf, reqn = k_a[:, 0:RT], k_a[:, RT:2 * RT]
            link(dve.tensor_copy(reqf, req[:, :]))
            link(dve.tensor_scalar(reqn, reqf, 0.0, float(NODES), ALU.is_lt, ALU.mult))
            link(dve.tensor_tensor(reqf, reqf, reqn, ALU.add))
            link(dve.tensor_scalar(req[:, :], reqf, 0.0, float(NODES - 1), ALU.max, ALU.min))

            a, b = k_a[:, 0:RT].bitcast(I32), k_a[:, RT:2 * RT].bitcast(I32)
            link(dve.tensor_scalar(a, io_r[:, :], -1.0, float(RT - 1 + (1 << 15)), ALU.mult, ALU.add))
            link(dve.tensor_scalar(b, a, KSHIFT, None, ALU.logical_shift_left))
            link(dve.tensor_tensor(a, b, req[:, :], ALU.bitwise_or))
            link(dve.tensor_scalar(k_a[:, RT:2 * RT], req[:, :], float(LAST), None, ALU.is_lt))
            link(dve.tensor_tensor(reqkey[:, :], k_a[:, 0:RT], k_a[:, RT:2 * RT], ALU.mult))
            link(dve.tensor_scalar(pbase[:, :], rowf[:, :], float(RT), float(RT - 1), ALU.mult, ALU.add))

            low = k_a[:, 0:RT].bitcast(I32)
            link(dve.tensor_scalar(low, req[:, :], P - 1, None, ALU.bitwise_and))
            link(dve.tensor_copy(rlo, low))
            link(dve.tensor_scalar(low, req[:, :], 7, None, ALU.logical_shift_right))
            link(dve.tensor_copy(rhi, low))
            one_hots(RT // TG, P, rlo, rhi, 0)
            link(dve.memset(mask[:, :], 0.0))
            dve.wait_ge(hist_mm, REQ_MM + 2)
            link(dve.tensor_scalar(mask[:, 0:BLOCKS], psum[7][:, 0:BLOCKS], 1.0, None, ALU.min))
            dve.sem_inc(const, 1)

            dve.wait_ge(edge_in, 32)
            low = k_a[0:EP, 0:EC].bitcast(I32)
            link(dve.tensor_scalar(low, dst_raw, P - 1, None, ALU.bitwise_and))
            link(dve.tensor_copy(dlo, low))
            link(dve.tensor_scalar(low, dst_raw, 7, None, ALU.logical_shift_right))
            link(dve.tensor_copy(dhi, low))
            one_hots(HB, EP, dlo, dhi, REQ_MM)
            dve.wait_ge(setup_mm, 5)
            link(dve.tensor_copy(maskt[:, :, :].rearrange("p n j -> p (n j)"), psum[6][:, 0:2 * P]))
            dve.sem_inc(const, 1)

            dve.wait_ge(hist_mm, REQ_MM + 2 + 2 * HB + 1)
            link(dve.tensor_scalar(deg[:, 0:BLOCKS], psum[7][:, 0:BLOCKS], 1.0, None, ALU.add))
            dve.sem_inc(deg_ready, 1)
            dve.wait_ge(root, 1)
            link(dve.reciprocal(dinv[:, :], nwt[:, :]))
            link(dve.tensor_tensor(nwt[:, :], dinv[:, :], dinv[:, :], ALU.mult))
            link(dve.tensor_tensor(nwt[:, :], nwt[:, :], deg[:, :], ALU.mult))
            link(dve.tensor_scalar(nwt[:, :], nwt[:, :], -0.5, 1.5, ALU.mult, ALU.add))
            link(dve.tensor_tensor(dinv[:, :], dinv[:, :], nwt[:, :], ALU.mult))

            dve.wait_ge(emb_in, 32)
            link(dve.tensor_tensor(acc3, acc3, dinv[:, :].unsqueeze(2).to_broadcast([P, PADB, F]), ALU.mult))
            dve.sem_inc(scaled, 1)

            up = k_a[0:EP, 0:EC].bitcast(I32)
            link(dve.tensor_scalar(up, dst_raw, float(OFF * P), None, ALU.add))
            link(dve.tensor_scalar(dst_raw, up, KSHIFT, None, ALU.logical_shift_left))
            link(dve.tensor_tensor(k_b[0:EP, :].bitcast(I32).rearrange("p (c j) -> p c j", j=COLS)[:, :, 0:CE],
                                   dst_raw.rearrange("p (c j) -> p c j", j=CE),
                                   src_raw.rearrange("p (c j) -> p c j", j=CE), ALU.bitwise_or))

            def signed(src, dst, k):
                a, b = (x.rearrange("p (g j) -> p g j", j=P) for x in (src, dst))
                dve.tensor_tensor(b, a, sgn_t[:, k:k + 1, :].to_broadcast([P, ALL // P, P]), ALU.mult).then_inc(k_stage, 1)

            def exchange(src, dst, stride):
                a, b = (x.rearrange("p (g t s) -> p g t s", t=2, s=stride) for x in (src, dst))
                dve.tensor_tensor(b[:, :, 0, :], a[:, :, 0, :], a[:, :, 1, :], ALU.min).then_inc(k_stage, 1)
                dve.tensor_tensor(b[:, :, 1, :], a[:, :, 0, :], a[:, :, 1, :], ALU.max).then_inc(k_stage, 1)

            def b3(x):
                return x.rearrange("p (b f) -> p b f", f=F)

            def node_stage(g):
                wait_if(dve, node_mm, g)
                d3 = dinv[:, g * BB:(g + 1) * BB].unsqueeze(2).to_broadcast([P, BB, F])
                dve.tensor_tensor(b3(stage), acc3[:, g * BB:(g + 1) * BB, :], d3, ALU.mult).then_inc(node_st, 1)

            def node_next(g):
                d3 = dinv[:, g * BB:(g + 1) * BB].unsqueeze(2).to_broadcast([P, BB, F])
                dve.wait_ge(node_mm, g + 1)
                dve.tensor_tensor(b3(tnode), b3(psum[6][:, :]), c12[:, :].unsqueeze(1).to_broadcast([P, BB, F]), ALU.add).then_inc(node_st, 1)
                dve.wait_ge(node_st, g * 3 + 3)
                dve.tensor_tensor(acc3[:, g * BB:(g + 1) * BB, :], b3(tnode), d3, ALU.mult).then_inc(node_st, 1)

            def sort(rnd, nodes_too):
                n = 0
                due = None
                for what, k, src, dst, before in steps:
                    if before:
                        dve.wait_ge(k_stage, rnd * SORT_STEPS + before)
                    if what == "sign":
                        signed(src, dst, k)
                    elif what == "exchange":
                        exchange(src, dst, k)
                        if due is not None:
                            node_next(due)
                            due = None
                    else:
                        if nodes_too:
                            node_stage(n)
                            due = n
                        n += 1
                        if what == "from_l":
                            for c in range(CHUNKS):
                                dve.wait_ge(tr_l, rnd * TO_L + (k - 8) * CHUNKS + c + 1)
                                dve.tensor_tensor(dst[:, c * COLS:(c + 1) * COLS], psum[c][:, 0:COLS],
                                                  sgn_l[:, k - 8, :], ALU.mult).then_inc(ev_l, 1)
                            dve.wait_ge(ev_l, rnd * (TO_L - CHUNKS) + (k - 7) * CHUNKS)
                        else:
                            dve.wait_ge(ev_t, rnd * TO_T + (k - 7) * CHUNKS)
                if nodes_too:
                    node_stage(n)
                rows = TILES // CHUNKS
                for c in range(CHUNKS):
                    dve.wait_ge(tr_l, rnd * TO_L + len(phases) * CHUNKS + c + 1)
                    link(dve.tensor_copy(skey.bitcast(F32).rearrange("p (r c) -> p r c", c=CHUNKS)[:, :, c], psum[c][:, 0:rows]))
                if nodes_too:
                    node_next(n)
                link(dve.tensor_scalar(sidx[:, :], skey, (1 << KSHIFT) - 1, None, ALU.bitwise_and))
                link(dve.tensor_scalar(sdst, skey, KSHIFT, None, ALU.logical_shift_right))
                tmp = k_a[:, 0:TILES].bitcast(I32)
                link(dve.tensor_scalar(tmp, skey, KSHIFT + 7, None, ALU.logical_shift_right))
                link(dve.tensor_scalar(sblk, tmp, float(BLOCKS - 1 + OFF), None, ALU.min))
                dve.sem_inc(prep, 1)
                for c in range(CHUNKS):
                    cut = slice(c * rows, (c + 1) * rows)
                    dve.wait_ge(bc, (2 * rnd) * CHUNKS + c + 1)
                    dve.tensor_scalar(blo[0:1, cut], psum[c][0:1, 0:rows], float(-OFF), None, ALU.add)
                    dve.scalar_tensor_tensor(out=rel[:, cut], in0=psum[c][:, 0:rows], scalar=float(-P), in1=sdst[:, cut],
                                             op0=ALU.mult, op1=ALU.add).then_inc(prep, 1)
                dve.wait_ge(prep, (rnd + 1) * (1 + CHUNKS))
                for c in range(CHUNKS):
                    cut = slice(c * rows, (c + 1) * rows)
                    dve.wait_ge(bc, (2 * rnd + 1) * CHUNKS + c + 1)
                    link(dve.scalar_tensor_tensor(out=span[0:1, cut], in0=psum[c][0:1, 0:rows], scalar=float(-OFF),
                                                  in1=blo[0:1, cut], op0=ALU.add, op1=ALU.subtract))
                link(dve.tensor_reduce(gspan[0:1, :], span[0:1, :].rearrange("p (g t) -> p g t", t=TG), AX.X, ALU.max))
                link(dve.tensor_scalar(valid[:, :], skey[0:1, :].bitcast(F32), PADKEY, None, ALU.is_lt))
                link(dve.tensor_reduce(vgrp[:, :], valid[:, :].rearrange("p (g t) -> p g t", t=TG), AX.X, ALU.max))
                link(dve.tensor_reduce(vgrp[:, 0:1], vgrp[:, :], AX.X, ALU.add))
                link(dve.tensor_scalar(ngrp[:, :], vgrp[:, 0:1], 1.0, None, ALU.max))
                dve.sem_inc(sorted_ready, 1)

            sort(0, False)

            for layer in range(2):
                base = layer * GROUPS
                if layer == 0:
                    dve.wait_ge(wanted_in, 16)
                with dve.Fori(0, groups_of(dve, layer)) as i:
                    most = dve.value_load(gspan[0:1, bass.ds(i, 1)], min_val=0, max_val=BLOCKS)
                    with dve.If(most >= W):
                        dve.wait_ge(added, (i + base) * TG + FREE_PS)
                        dve.sem_inc(held, 1)
                        with dve.Fori(0, TG) as u:
                            s = dve.value_load(span[0:1, bass.ds(i * TG + u, 1)], min_val=0, max_val=BLOCKS)
                            with dve.If(s >= W):
                                first = dve.value_load(blo[0:1, bass.ds(i * TG + u, 1)], min_val=0, max_val=BLOCKS - 1)
                                chain.add()
                                dve.tensor_scalar(xdst[:, :], skey[:, bass.ds(i * TG + u, 1)], KSHIFT, None,
                                                  ALU.logical_shift_right).then_inc(x_chain, 1)
                                dve.wait_ge(x_chain, chain.value())
                                chain.add()
                                dve.tensor_copy(xdsf[:, :], xdst[:, :]).then_inc(x_chain, 1)
                                dve.wait_ge(x_chain, chain.value())
                                dve.sem_inc(held, 1)
                                with dve.Fori(W, s + 1) as j:
                                    visits.add()
                                    dve.reg_add(blk_reg, first, j)
                                    at_blk = dve.snap(blk_reg, min_val=0, max_val=BLOCKS - 1)
                                    dve.tensor_scalar(xoh[:, :], colf[:, :], xblk[:, bass.ds(at_blk, 1)], xdsf[:, 0:1],
                                                      ALU.add, ALU.is_equal).then_inc(x_oh, 1)
                                    dve.wait_ge(x_mm, visits.value())
                                    rows_of = acc[:, bass.ds(at_blk * F, F)]
                                    chain.add()
                                    dve.tensor_tensor(rows_of, psum[4][:, 0:F], rows_of, ALU.add).then_inc(x_chain, 1)
                                    dve.wait_ge(x_chain, chain.value())
                                dve.nop()
                            dve.nop()
                        dve.nop()
                    for u in range(TG):
                        if u % HT == 0:
                            if layer == 0:
                                dve.wait_ge(flagged, i * TG + (u + 1))
                            dve.tensor_tensor(ohw, iorep[:, :, :],
                                              rel[:, bass.ds(i * TG + u, HT)].unsqueeze(1).to_broadcast([P, W * P, HT]),
                                              ALU.is_equal).then_inc(oh_ready, 1)
                            firsts = load_row(dve, blo[0:1, bass.ds(i * TG + u, HT)], BLOCKS - 1)
                        if layer == 0 and u == 4:
                            dve.wait_ge(taken, i * 2 + 1)
                            dve.wait_ge(comp_done, i + 1)
                            dve.sem_inc(held, 1)
                            dve.max(top8[:, :], reqkey[:, :]).then_inc(taken, 1)
                        if layer == 0 and u == 8:
                            dve.wait_ge(taken, i * 2 + 2)
                            dve.sem_inc(held, 1)
                            dve.match_replace(reqkey[:, :], top8[:, :], reqkey[:, :], 0.0).then_inc(taken, 1)
                        first = firsts[u % HT]
                        dve.wait_ge(mm_done, (i + base) * TG + (u + 1 + FREE_MM))
                        dve.wait_ge(added, (i + base) * TG + (u + FREE_PS))
                        window = acc[:, bass.ds(first * F, W * F)]
                        dve.tensor_tensor(window, psum[u % NPS][:, 0:W * F], window, ALU.add).then_inc(added, 1)
                        if layer == 0:
                            dve.wait_ge(flagged, i * TG + (u + 1))
                            dve.scalar_tensor_tensor(
                                out=junk[:, :], in0=ohw[:, :, u % HT], scalar=1.0,
                                in1=wanted[:, bass.ds(first * P, W * P)], op0=ALU.mult, op1=ALU.mult,
                                accum_out=keep[:, bass.ds(i * TG + u, 1)]).then_inc(flagged, 1)

                if layer == 0:
                    dve.wait_ge(added, GROUPS * TG + FREE_PS)
                    dve.wait_ge(flagged, GROUPS * TG + 1)
                    dve.sem_inc(node_st, 1)
                    dve.wait_ge(comp_done, GROUPS + 1)
                    cb = comp[:, 0:RCOLS].bitcast(I32)
                    t0, t1 = k_a[:, 0:RCOLS], k_a[:, RCOLS:2 * RCOLS]
                    link(dve.tensor_scalar(ccol[:, 0, :], cb, (1 << KSHIFT) - 1, None, ALU.bitwise_and))
                    link(dve.tensor_scalar(t0.bitcast(I32), cb, KSHIFT, 1023, ALU.logical_shift_right, ALU.bitwise_and))
                    link(dve.tensor_scalar(t1, t0.bitcast(I32), -1.0, pbase[:, 0:1], ALU.mult, ALU.add))
                    link(dve.tensor_scalar(t0, comp[:, 0:RCOLS], 0.0, float(1 << 20), ALU.is_equal, ALU.mult))
                    link(dve.tensor_tensor(ccol[:, 1, :], t0, t1, ALU.add))
                    link(dve.tensor_scalar(t0, comp[:, 0:RCOLS], 0.0, None, ALU.is_gt))
                    link(dve.tensor_reduce(cnt[:, :], t0, AX.X, ALU.add))
                    dve.sem_inc(counts_in, 1)
                    dve.wait_ge(count_tr, 1)
                    link(dve.tensor_reduce(nrf[:, 0:1], psum[7][0:1, 0:P], AX.X, ALU.max))
                    link(dve.tensor_copy(nreq[:, 0:1], nrf[:, 0:1]))
                    link(dve.tensor_scalar(nrf[:, 1:1 + RCOLS // ROUND], io_r[0:1, 0:RCOLS // ROUND], float(ROUND), nrf[:, 0:1],
                                           ALU.mult, ALU.is_lt))
                    link(dve.tensor_reduce(nrf[:, 7:8], nrf[:, 1:1 + RCOLS // ROUND], AX.X, ALU.add))
                    link(dve.tensor_scalar(nreq[:, 1:2], nrf[:, 7:8], 1.0, None, ALU.max))
                    dve.sem_inc(counts, 1)
                    far = k_a[:, 0:TILES]
                    link(dve.tensor_scalar(far, rel, float(W * P), None, ALU.is_ge))
                    link(dve.tensor_tensor(keep[:, :], keep[:, :], far, ALU.max))
                    link(dve.memset(k_b, PADKEY))
                    link(dve.copy_predicated(k_b.rearrange("p (c j) -> p j c", c=CHUNKS)[:, 0:TILES // CHUNKS, :],
                                             keep[:, :].bitcast(I32).rearrange("p (j c) -> p j c", c=CHUNKS),
                                             skey.bitcast(F32).rearrange("p (j c) -> p j c", c=CHUNKS)))
                    sort(1, True)

            dve.wait_ge(added, (groups_of(dve, 1) + GROUPS) * TG + FREE_PS)
            for n, (blk0, blk1) in enumerate([(FULLB, BLOCKS)] + PIECES):
                m = blk1 - blk0
                if n == 1:
                    dve.wait_ge(last_in, 16)
                    link(dve.tensor_copy(fill.rearrange("p (t f) -> p t f", f=F), lrow[:, :].unsqueeze(1).to_broadcast([P, FILL, F])))
                    dve.sem_inc(fill_ready, 1)
                link(dve.tensor_tensor(acc3[:, blk0:blk1, :], acc3[:, blk0:blk1, :], dinv[:, blk0:blk1].unsqueeze(2).to_broadcast([P, m, F]), ALU.mult))
                link(dve.tensor_tensor(acc3[:, blk0:blk1, :], acc3[:, blk0:blk1, :], b2r[:, :].unsqueeze(1).to_broadcast([P, m, F]), ALU.add))
                dve.sem_inc(rows_ready, 1)


_INS = ["r_input", "L0_rec_emb", "L0_rec_W1", "L0_rec_b1", "L0_rec_W2", "L0_rec_b2", "L0_rec_edge_index"]


def kernel(**inputs):
    import numpy as np
    import concourse.bacc as bacc
    from concourse.bass_utils import run_bass_kernel_spmd

    nc = bacc.Bacc("TRN2", target_bir_lowering=False, num_devices=1)
    arrays, args = {}, []
    for name in _INS:
        a = np.ascontiguousarray(inputs[name])
        arrays["in_" + name] = a
        args.append(nc.dram_tensor("in_" + name, a.shape, mybir.dt.from_np(a.dtype), kind="ExternalInput").ap())
    out = nc.dram_tensor("out", (BATCH, SEQ, F), F32, kind="ExternalOutput").ap()
    gcn_program(nc, *args, out)
    r = run_bass_kernel_spmd(nc, [arrays], core_ids=[0])
    return r.results[0]["out"]
```

```python
from contextlib import ExitStack

import concourse.bass as bass
from concourse import mybir

ALU = mybir.AluOpType
ACT = mybir.ActivationFunctionType
AX = mybir.AxisListType
F32 = mybir.dt.float32
BF16 = mybir.dt.bfloat16
I32 = mybir.dt.int32
I16 = mybir.dt.int16

P = 128
NODES, F, HID, EDGES = 18750, 64, 128, 300000
BATCH, SEQ = 512, 200
REQS = BATCH * SEQ
RT = REQS // P
LAST = NODES - 1
OG = 10
QG = 14
ROUND = OG * QG
RCOLS = -(-RT // ROUND) * ROUND
FILL = 25

BLOCKS = -(-NODES // P)
BB = 8
NBATCH = 19
PADB = BB * NBATCH
FULLB = NODES // P
TAIL = NODES - FULLB * P
PARTS = 3
ROW = PARTS * F

CHUNKS, SB = 5, 16
COLS = (1 << SB) // P
ALL = CHUNKS * COLS
EP = 125
EC = EDGES // EP
CE = EC // CHUNKS
OFF = 2
KSHIFT = 15
PADKEY = float(2 ** 127)
TG = 20
HT = TG // 2
GROUPS = -(-(-(-EC * EP // CHUNKS // P)) * CHUNKS // TG)
TILES = GROUPS * TG
W = 2
HALVES = EC // HT
HU = 6


def gcn_program(nc, r_input, emb, w1, b1, w2, b2, edges, out):
    table = nc.dram_tensor("table", (PADB * P, ROW), BF16, kind="Internal").ap()
    marks = nc.dram_tensor("marks", (2 * P, P), BF16, kind="Internal").ap()
    last = nc.dram_tensor("last", (1, F), F32, kind="Internal").ap()
    nodes = nc.dram_tensor("nodes", (NODES, F), F32, kind="Internal").ap()

    ctx = ExitStack()
    with ctx:
        def sb(name, shape, dt):
            return ctx.enter_context(nc.sbuf_tensor(name, shape, dt))

        def sem(name):
            return ctx.enter_context(nc.semaphore(name))

        acc = sb("acc", [P, PADB * F], F32)
        acc3 = acc[:, :].rearrange("p (b f) -> p b f", f=F)
        raw = sb("raw", [P, 3 * EC], I32)
        dst_raw, src_raw = raw[0:EP, 0:EC], raw[0:EP, EC:2 * EC]
        dlo = raw[0:EP, 2 * EC:2 * EC + EC // 2].bitcast(BF16)
        dhi = raw[0:EP, 2 * EC + EC // 2:3 * EC].bitcast(BF16)
        skey = raw[:, 0:TILES]
        sidx = sb("sidx", [P, TILES], I32)
        sdst = raw[:, EC:EC + TILES]
        rel = raw[:, 2 * EC:2 * EC + TILES // 2].bitcast(BF16)
        work = sb("work", [P, PADB * P // 2], F32)
        wanted = work[:, :].bitcast(BF16)
        cut = [0]

        def carve(n):
            cut[0] += n
            return work[:, cut[0] - n:cut[0]]

        k_a, k_b = carve(ALL), carve(ALL)
        stage, zt, tnode = carve(BB * F), carve(BB * F), carve(BB * F)
        res = carve(2 * BB * F).rearrange("p (n f) -> p n f", n=2)
        tab = carve(BB * ROW).bitcast(BF16).rearrange("p (s b f) -> p s b f", s=2, f=ROW)
        nlo = work[0:EP, 2 * ALL:2 * ALL + EC]
        sgn_t = sb("sgn_t", [P, 7, P], BF16)
        sgn_l = sb("sgn_l", [P, SB - 7, COLS], BF16)
        io_r = sb("io_r", [P, RT], I32)
        it_i = io_r[:, 0:COLS]
        it_y = sb("it_y", [P, 1], I32)
        iorep = sb("iorep", [P, W * P, HT], BF16)
        oh = sb("oh", [P, 2, (P + BLOCKS) * HT], BF16)
        ohw = oh[:, 0, 0:W * P * HT].rearrange("p (j t) -> p j t", t=HT)
        ring = sb("ring", [P, TG, ROW], BF16)
        gidx = sb("gidx", [P, TG], I32)
        keep = sb("keep", [P, TILES], F32)
        junk = sb("junk", [P, W * P], BF16)
        vsum = sb("vsum", [1, 1], F32)
        vgrp = sb("vgrp", [1, GROUPS], F32)
        vrow = sb("vrow", [1, CHUNKS, GROUPS], F32)
        ngrp = sb("ngrp", [1, 1], I32)
        mask = sb("mask", [P, 2 * P], F32)
        maskt = sb("maskt", [P, 2, P], BF16)
        rlo, rhi = (keep[:, n * (RT // 2):(n + 1) * (RT // 2)].bitcast(BF16) for n in range(2))
        blo = sb("blo", [1, TILES], I16)
        span = sb("span", [1, TILES], I16)
        gspan = sb("gspan", [1, GROUPS], I16)
        dinv = sb("dinv", [P, PADB], F32)
        deg = sb("deg", [P, PADB], F32)
        nwt = sb("nwt", [P, PADB], F32)
        steps_oh = sb("steps_oh", [P, 2, P * HT], BF16)
        first_sign = sb("first_sign", [EP, 1], F32)
        diff = sb("diff", [P, P], F32)
        stepsum = sb("stepsum", [P, BLOCKS], F32)
        colf = sb("colf", [P, P], F32)
        rowf = sb("rowf", [P, 1], F32)
        ident = sb("ident", [P, P], F32)
        ident_h = sb("ident_h", [P, P], BF16)
        ones = sb("ones", [P, P], BF16)
        ends = sb("ends", [P, 2, ALL // P], F32)
        ends_i = sb("ends_i", [P, 2, ALL // P], I32)
        ends_b = sb("ends_b", [P, 2, ALL // P], BF16)
        zero = sb("zero", [P, BLOCKS], BF16)
        zf = sb("zf", [P, P], F32)
        w1s = sb("w1s", [F, HID], F32)
        w1t = sb("w1t", [HID, P], F32)
        w2s = sb("w2s", [HID, F], F32)
        b1s = sb("b1s", [HID, 1], F32)
        b1r = sb("b1r", [HID, P], F32)
        b2r = sb("b2r", [P, F], F32)
        w12 = sb("w12", [P, P], F32)
        c12 = sb("c12", [P, F], F32)
        req = sb("req", [P, RT], I32)
        oidx = sb("oidx", [P, 2, ROUND], I32)
        reqkey = sb("reqkey", [P, RT], F32)
        top8 = sb("top8", [P, 8], F32)
        comp = sb("comp", [P, GROUPS * 8], F32)
        ccol = sb("ccol", [P, 2, RCOLS], I32)
        cnt = sb("cnt", [P, 1], F32)
        nreq = sb("nreq", [1, 2], I32)
        nrf = sb("nrf", [1, 8], F32)
        pbase = sb("pbase", [P, 1], F32)
        odd = sb("odd", [P, 1], F32)
        odd_i = sb("odd_i", [P, 1], I32)
        lrow = sb("lrow", [P, F], F32)
        fill = k_a[:, 0:FILL * F]
        xblk = sb("xblk", [P, PADB], F32)
        xdst = sb("xdst", [P, 1], I32)
        xdsf = sb("xdsf", [P, 1], F32)
        xoh = sb("xoh", [P, P], BF16)

        psum = [ctx.enter_context(nc.psum_tensor(f"ps{i}", [P, 512], F32)) for i in range(8)]

        marks_out = sem("marks_out")
        wanted_in = sem("wanted_in")
        emb_in = sem("emb_in")
        edge_in = sem("edge_in")
        w_in = sem("w_in")
        req_in = sem("req_in")
        iotas = sem("iotas")
        const = sem("const")
        hist_oh = sem("hist_oh")
        hist_mm = sem("hist_mm")
        hist_steps = sem("hist_steps")
        nlo_ready = sem("nlo_ready")
        counted = sem("counted")
        step = sem("step")
        deg_steps = sem("deg_steps")
        deg_ready = sem("deg_ready")
        root = sem("root")
        scaled = sem("scaled")
        part_act = sem("part_act")
        part_pool = sem("part_pool")
        tab_out = [sem(f"tab_out{s}") for s in range(2)]
        stage_done = sem("stage_done")
        k_stage = sem("k_stage")
        tr_l = sem("tr_l")
        tr_t = sem("tr_t")
        ev_l = sem("ev_l")
        ev_t = sem("ev_t")
        prep = sem("prep")
        bc = sem("bc")
        keys_read = sem("keys_read")
        sources_ready = sem("sources_ready")
        sorted_ready = sem("sorted_ready")
        idx_ready = sem("idx_ready")
        gathered = [sem(f"gathered{u}") for u in range(TG)]
        oh_ready = sem("oh_ready")
        mm_done = sem("mm_done")
        added = sem("added")
        flagged = sem("flagged")
        x_oh = sem("x_oh")
        x_mm = sem("x_mm")
        x_chain = sem("x_chain")
        held = sem("held")
        setup_mm = sem("setup_mm")
        node_st = sem("node_st")
        node_tr = sem("node_tr")
        node_zt = sem("node_zt")
        node_mm = sem("node_mm")
        rows_ready = sem("rows_ready")
        nodes_out = sem("nodes_out")
        taken = sem("taken")
        comp_done = sem("comp_done")
        counts = sem("counts")
        counts_in = sem("counts_in")
        count_tr = sem("count_tr")
        last_out = sem("last_out")
        last_in = sem("last_in")
        fill_ready = sem("fill_ready")
        filled = sem("filled")
        out_idx = sem("out_idx")
        round_done = sem("round_done")
        got = [sem(f"got{q}") for q in range(QG)]
        put = [sem(f"put{q}") for q in range(QG)]

        block = ctx.enter_context(nc.Block())

        def batches(eng, body):
            for s in range(2):
                body(s, s, 0)
            with eng.Fori(1, NBATCH // 2) as i:
                for s in range(2):
                    body(i * 2 + s, s, i)
            body(NBATCH - 1, 0, NBATCH // 2)

        TURN_HALVES = [3 if n % 2 else 2 for n in range(16)]
        R1 = sum(TURN_HALVES)
        R0 = RT // HT - R1
        OH_STEP = 2 * HU - HU // 3
        assert R0 % 2 == 0 and R0 > 0
        FREE_MM, FREE_PS = TG, 4
        NPS = 4
        PIECES = [(0, 37), (37, 74), (74, 110), (110, FULLB)]

        phases = range(8, SB + 1)
        steps = [("sign", 0, k_b, k_a, 0)]
        turns = []
        turned = []
        done, cur, other = 1, k_a, k_b
        for k in range(1, SB + 1):
            if 1 < k < 8:
                steps.append(("sign", k - 1, cur, other, done))
                done, cur, other = done + 1, other, cur
            for bit in range(k - 1, 6 if k == SB else -1, -1):
                fresh = k >= 8 and bit in (k - 1, 6)
                if fresh:
                    turns.append((done, cur))
                    cur, other = other, cur
                    steps.append(("from_l" if bit == k - 1 else "from_t", k, None, cur, 0))
                    if bit == 6:
                        turned.append(cur)
                stride = 1 << (bit - 7 if bit >= 7 else bit)
                steps.append(("exchange", stride, cur, other, 0 if fresh else done))
                done, cur, other = done + 2, other, cur
        turns.append((done, cur))
        final = cur
        SORT_STEPS = done
        TO_L = TO_T = len(turns) // 2 * CHUNKS
        EV_T = len(turned) * CHUNKS

        def turn(pe, src, signal):
            for c in range(CHUNKS):
                for q in range(COLS // P):
                    mm = pe.transpose(psum[c][:, q * P:(q + 1) * P],
                                      src[:, c * COLS + q * P:c * COLS + (q + 1) * P], ident[:, :])
                mm.then_inc(signal, 1)

        def load_row(eng, ap, most):
            return nc.values_load_multi_w_load_instructions(
                ap, engines=[eng.engine], min_val=0, max_val=most,
                skip_runtime_bounds_check_because="the rows hold clamped block numbers")[1]

        def wait_if(eng, signal, value):
            if not (isinstance(value, int) and value == 0):
                eng.wait_ge(signal, value)

        def peeled(eng, n, body):
            body(0)
            with eng.Fori(1, n) as i:
                body(i)

        def groups_of(eng, layer):
            return eng.value_load(ngrp[0:1, 0:1], min_val=1, max_val=GROUPS) if layer else GROUPS

        class Count:

            def __init__(self, eng, name):
                self.eng, self.reg = eng, eng.alloc_register(name)
                eng.reg_mov(self.reg, 0)

            def add(self):
                self.eng.reg_add(self.reg, self.reg, 1)

            def value(self):
                return self.eng.snap(self.reg, min_val=0, max_val=1 << 24)

        @block.sync
        def _(sp):
            sp.dma_start(dst_raw, edges[1].rearrange("(p j) -> p j", p=EP)).then_inc(edge_in, 16)
            sp.dma_start(src_raw, edges[0].rearrange("(p j) -> p j", p=EP)).then_inc(edge_in, 16)
            sp.dma_start(w1s[:, :], w1).then_inc(w_in, 16)
            sp.dma_start(w2s[:, :], w2).then_inc(w_in, 16)
            sp.dma_start(b1s[:, :], b1.rearrange("(h a) -> h a", a=1)).then_inc(w_in, 16)
            sp.dma_start(b2r[:, :], b2.rearrange("(a f) -> a f", a=1).to_broadcast([P, F])).then_inc(w_in, 16)
            sp.dma_start(req[:, :], r_input.rearrange("a b -> (a b)").rearrange("(p t) -> p t", p=P)).then_inc(req_in, 16)
            sp.wait_ge(const, 1)
            sp.dma_start(acc3[:, 0:FULLB, :], emb[0:FULLB * P, :].rearrange("(b p) f -> p b f", p=P)).then_inc(emb_in, 16)
            sp.dma_start(acc3[0:TAIL, FULLB, :], emb[FULLB * P:NODES, :]).then_inc(emb_in, 16)

            for layer in range(2):
                def store(g, s, i):
                    sp.wait_ge(part_act, PARTS * (g + 1 + layer * NBATCH))
                    rows = table[bass.ds(g * (BB * P), BB * P), :].rearrange("(b p) f -> p b f", p=P)
                    sp.dma_start(rows, tab[:, s]).then_inc(tab_out[s], 16)
                batches(sp, store)
                if layer == 0:
                    sp.wait_ge(const, 5)
                    sp.dma_start(marks.rearrange("(n p) j -> p n j", p=P), maskt[:, :, :]).then_inc(marks_out, 16)
                    sp.wait_ge(marks_out, 16)
                    sp.wait_ge(tr_t, TO_T)
                    sp.wait_ge(keys_read, 1)
                    sp.wait_ge(tab_out[0], 16 * (NBATCH // 2 + 1))
                    sp.wait_ge(tab_out[1], 16 * (NBATCH // 2))
                    sp.dma_start(wanted, marks.rearrange("(a n) j -> a (n j)", a=1)[:, 0:PADB * P].to_broadcast([P, PADB * P])).then_inc(wanted_in, 16)

            sp.wait_ge(rows_ready, 1)
            sp.dma_start(last, acc3[(LAST % P):(LAST % P) + 1, LAST // P, :]).then_inc(last_out, 16)
            sp.wait_ge(last_out, 16)
            sp.dma_start(lrow[:, :], last.to_broadcast([P, F])).then_inc(last_in, 16)
            for n, (blk0, blk1) in enumerate(PIECES):
                sp.wait_ge(rows_ready, n + 2)
                sp.dma_start(nodes[blk0 * P:blk1 * P, :].rearrange("(b p) f -> p b f", p=P), acc3[:, blk0:blk1, :]).then_inc(nodes_out, 16)
            sp.dma_start(nodes[FULLB * P:NODES, :], acc3[0:TAIL, FULLB, :]).then_inc(nodes_out, 16)

            rows = out.rearrange("a b f -> (a b) f").rearrange("(p r t) f -> p r (t f)", p=P, t=FILL)
            sp.wait_ge(fill_ready, 1)
            sp.dma_start(rows, fill.unsqueeze(1).to_broadcast([P, RT // FILL, FILL * F])).then_inc(filled, 16)
            sp.wait_ge(filled, 16)

        @block.gpsimd
        def _(pool):
            pool.iota(io_r[:, :], pattern=[[1, RT]], base=0, channel_multiplier=0).then_inc(iotas, 1)
            pool.iota(it_y[:, 0:1], pattern=[[1, 1]], base=0, channel_multiplier=1).then_inc(iotas, 1)
            pool.iota(iorep[:, :, :], pattern=[[1, W * P], [0, HT]], base=0, channel_multiplier=0,
                      allow_small_or_imprecise_dtypes=True).then_inc(iotas, 1)
            for k in range(SB):
                dst, bits, q = (sgn_t[:, k, :], 7, k) if k < 7 else (sgn_l[:, k - 7, :], SB - 7, k - 7)
                pattern = [[0, 1 << (bits - 2 - q)], [1, 2], [1, 2]] if q < bits - 1 else [[1, 2]]
                if k == 0:
                    pattern[2] = [0, 2]
                if q:
                    pattern = pattern + [[0, 1 << q]]
                pool.iota(dst, pattern=[d for d in pattern if d[1] > 1], base=0, channel_multiplier=0,
                          allow_small_or_imprecise_dtypes=True).then_inc(iotas, 1)

            for layer in range(2):
                def rest(g, s, i):
                    b = g + layer * NBATCH
                    x = acc[:, bass.ds(g * (BB * F), BB * F)].rearrange("p (b f) -> p b f", f=F)
                    r = [res[:, n, :].rearrange("p (b f) -> p b f", f=F) for n in range(2)]
                    pool.wait_ge(part_act, b * PARTS + 1)
                    pool.tensor_tensor(r[0], x, tab[:, s, :, 0:F], ALU.subtract).then_inc(part_pool, 1)
                    pool.wait_ge(part_pool, b * 2 + 1)
                    pool.wait_ge(part_act, b * PARTS + 2)
                    pool.tensor_tensor(r[1], r[0], tab[:, s, :, F:2 * F], ALU.subtract).then_inc(part_pool, 1)
                batches(pool, rest)

                pool.wait_ge(tab_out[0], 16 * (NBATCH // 2 + 1) * (layer + 1))
                pool.wait_ge(tab_out[1], 16 * (NBATCH // 2) * (layer + 1))
                if layer:
                    pool.wait_ge(sources_ready, layer + 1)
                with pool.Fori(0, groups_of(pool, layer)) as i:
                    for u in range(TG):
                        if u % HT == 0:
                            pool.wait_ge(idx_ready, (i + layer * GROUPS) * 2 + (u // HT + 1))
                            pool.sem_inc(held, 1)
                        pool.indirect_dma_start(
                            out=ring[:, u, :], out_offset=None, in_=table,
                            in_offset=bass.IndirectOffsetOnAxis(ap=gidx[:, u:u + 1], axis=0)).then_inc(gathered[u], 16)

            result = out.rearrange("a b f -> (a b) f")
            pool.wait_ge(counts, 1)
            most = pool.value_load(nreq[0:1, 0:1], min_val=0, max_val=RT)
            rounds = pool.value_load(nreq[0:1, 1:2], min_val=1, max_val=RCOLS // ROUND)
            pool.sem_inc(round_done, 1)
            pool.wait_ge(nodes_out, 16 * (len(PIECES) + 1))
            with pool.Fori(0, rounds) as r:
                pool.wait_ge(out_idx, r + 1)
                pool.sem_inc(held, 1)
                for q in range(QG):
                    with pool.If(most > r * ROUND + q * OG):
                        for t in range(q * OG, (q + 1) * OG):
                            pool.indirect_dma_start(
                                out=acc[:, t * F:(t + 1) * F], out_offset=None, in_=nodes,
                                in_offset=bass.IndirectOffsetOnAxis(ap=oidx[:, 0, t:t + 1], axis=0)).then_inc(got[q], 16)
                pool.wait_ge(filled, 16)
                for q in range(QG):
                    with pool.If(most > r * ROUND + q * OG):
                        pool.wait_ge(got[q], (r + 1) * (16 * OG))
                        pool.sem_inc(held, 1)
                        for t in range(q * OG, (q + 1) * OG):
                            pool.indirect_dma_start(
                                out=result, out_offset=bass.IndirectOffsetOnAxis(ap=oidx[:, 1, t:t + 1], axis=0),
                                in_=acc[:, t * F:(t + 1) * F], in_offset=None,
                                bounds_check=REQS - 1, oob_is_err=False).then_inc(put[q], 16)
                for q in range(QG):
                    with pool.If(most > r * ROUND + q * OG):
                        pool.wait_ge(put[q], (r + 1) * (16 * OG))
                        pool.sem_inc(held, 1)
                pool.sem_inc(round_done, 1)

        @block.scalar
        def _(act):
            act.sem_inc(comp_done, 1)
            act.wait_ge(nlo_ready, 1)
            act.activation(first_sign[:, :], nlo[:, 0:1], ACT.Sign)
            with act.Fori(0, HALVES // HU) as i:
                for s in range(HU // 3):
                    act.wait_ge(hist_mm, i * HU + (R0 + 3 * s - 1))
                    for t in range(HT):
                        last_step = act.activation(steps_oh[0:EP, s, t * P:(t + 1) * P], colf[0:EP, :], ACT.Sign,
                                                   bias=nlo[:, bass.ds(i * (HU * HT) + ((3 * s + 2) * HT + t), 1)])
                    last_step.then_inc(hist_steps, 1)
            act.wait_ge(deg_ready, 1)
            act.activation(nwt[:, :], deg[:, :], ACT.Sqrt).then_inc(root, 1)

            for layer in range(2):
                def parts(g, s, i):
                    b = g + layer * NBATCH
                    x = acc[:, bass.ds(g * (BB * F), BB * F)].rearrange("p (b f) -> p b f", f=F)
                    r = [res[:, n, :].rearrange("p (b f) -> p b f", f=F) for n in range(2)]
                    if layer == 0:
                        act.wait_ge(scaled, 1)
                    else:
                        act.wait_ge(node_st, 1 + g * 3 + 3)
                    if layer == 0:
                        wait_if(act, tab_out[s], i * 16)
                    else:
                        act.wait_ge(tab_out[s], (i + (NBATCH // 2 + 1 - s)) * 16)
                    act.activation(tab[:, s, :, 0:F], x, ACT.Copy).then_inc(part_act, 1)
                    act.wait_ge(part_pool, b * 2 + 1)
                    act.activation(tab[:, s, :, F:2 * F], r[0], ACT.Copy).then_inc(part_act, 1)
                    act.wait_ge(part_pool, b * 2 + 2)
                    act.activation(tab[:, s, :, 2 * F:3 * F], r[1], ACT.Copy).then_inc(part_act, 1)

                def nodes_t(g):
                    act.wait_ge(node_tr, g + 1)
                    act.activation(zt[:, :], psum[5][:, :], ACT.Copy).then_inc(node_zt, 1)
                    parts(g, g % 2, g // 2)

                if layer == 0:
                    batches(act, parts)
                else:
                    nodes_t(0)
                    nodes_t(1)
                for n, dst in enumerate(turned):
                    for c in range(CHUNKS):
                        act.wait_ge(tr_t, layer * TO_T + n * CHUNKS + c + 1)
                        act.activation(dst[:, c * COLS:(c + 1) * COLS], psum[c][:, 0:COLS], ACT.Copy).then_inc(ev_t, 1)
                    if layer:
                        nodes_t(2 * n + 2)
                        nodes_t(2 * n + 3)
                if layer:
                    nodes_t(NBATCH - 1)

                act.wait_ge(sources_ready, layer + 1)
                with act.Fori(0, groups_of(act, layer)) as i:
                    for h in range(2):
                        act.wait_ge(mm_done, (i + layer * GROUPS) * TG + (h + 1) * HT)
                        act.copy(gidx[:, h * HT:(h + 1) * HT],
                                 sidx[:, bass.ds(i * TG + h * HT, HT)]).then_inc(idx_ready, 1)
                    if layer == 0:
                        act.wait_ge(taken, i * 2 + 2)
                        act.copy(comp[:, bass.ds(i * 8, 8)], top8[:, :]).then_inc(comp_done, 1)

            act.wait_ge(counts, 1)
            rounds = act.value_load(nreq[0:1, 1:2], min_val=1, max_val=RCOLS // ROUND)
            with act.Fori(0, rounds) as r:
                act.wait_ge(round_done, r + 1)
                act.copy(oidx[:, :, :], ccol[:, :, bass.ds(r * ROUND, ROUND)]).then_inc(out_idx, 1)

        @block.tensor
        def _(pe):
            visits = Count(pe, "pe_visits")

            def sort_turns(rnd, between):
                for n, (ready, src) in enumerate(turns):
                    pe.wait_ge(k_stage, rnd * SORT_STEPS + ready)
                    if n % 2:
                        pe.wait_ge(ev_l, rnd * TO_L + (n + 1) // 2 * CHUNKS)
                    elif n + rnd:
                        pe.wait_ge(ev_t, rnd * EV_T + n // 2 * CHUNKS)
                    turn(pe, src, tr_t if n % 2 else tr_l)
                    if between:
                        between(n)

            def tile_blocks(rnd):
                for e in range(2):
                    pe.wait_ge(prep, rnd * (1 + CHUNKS) + 1 + e * CHUNKS)
                    for c in range(CHUNKS):
                        for q in range(COLS // P):
                            g = c * (COLS // P) + q
                            mm = pe.matmul(psum[c][:, q * P:(q + 1) * P], ends_b[:, e, g:g + 1].to_broadcast([P, P]),
                                           ident_h[:, :], start=True, stop=True)
                        mm.then_inc(bc, 1)

            pe.sem_inc(mm_done, FREE_MM)
            pe.sem_inc(hist_mm, 2)
            pe.wait_ge(const, 2)
            pe.wait_ge(w_in, 64)
            pe.transpose(psum[6][:, 0:F], w1s[:, :], ident[0:F, 0:F]).then_inc(setup_mm, 1)
            pe.wait_ge(const, 3)
            pe.matmul(psum[5][:, 0:F], w1t[:, :], w2s[:, :], start=True, stop=True).then_inc(setup_mm, 1)
            pe.matmul(psum[4][:, 0:F], b1r[:, :], w2s[:, :], start=True, stop=True).then_inc(setup_mm, 1)

            def count_half(bank, parts, h, n, steps=None):
                blk = oh[0:parts, h, P * HT:].rearrange("p (j t) -> p j t", t=HT)
                if steps is None:
                    lane = oh[0:parts, h, 0:P * HT].rearrange("p (j t) -> p j t", t=HT)
                else:
                    lane = steps_oh[0:parts, steps, :].rearrange("p (t j) -> p j t", j=P)
                pe.wait_ge(hist_oh, n)
                for t in range(HT):
                    mm = pe.matmul(bank[:, 0:BLOCKS], lane[:, :, t], blk[:, :, t], start=False, stop=False)
                mm.then_inc(hist_mm, 1)

            def count_end(bank):
                pe.matmul(bank[:, 0:BLOCKS], ones[:, :], zero[:, :], start=False, stop=True).then_inc(counted, 1)

            def count_start(bank):
                pe.matmul(bank[:, 0:BLOCKS], ones[:, :], zero[:, :], start=True, stop=False)

            count_start(psum[6])
            with pe.Fori(0, R0 // 2) as i:
                for h in range(2):
                    count_half(psum[6], P, h, i * 4 + (2 * h + 2))
            pe.wait_ge(hist_oh, 2 * R0 + 1)
            count_start(psum[5])
            count_start(psum[7])
            with pe.Fori(0, HALVES // HU) as i:
                for m in range(HU):
                    ready = i * OH_STEP + (2 * R0 + 2 * (m + 1) - (m + 1) // 3)
                    if m % 3 == 2:
                        pe.wait_ge(hist_steps, i * 2 + (m // 3 + 1))
                        count_half(psum[5], EP, m % 2, ready, m // 3)
                    else:
                        count_half(psum[7], EP, m % 2, ready)
            count_end(psum[5])
            count_end(psum[7])
            pe.wait_ge(deg_steps, 1)
            pe.matmul(psum[4][:, 0:BLOCKS], diff[:, :], stepsum[:, :], start=True, stop=True).then_inc(setup_mm, 1)

            def requests(n):
                if n < len(TURN_HALVES):
                    for m in range(sum(TURN_HALVES[:n]), sum(TURN_HALVES[:n + 1])):
                        count_half(psum[6], P, m % 2, 2 * (R0 + m + 1) + HALVES // HU * OH_STEP)
                    if n == len(TURN_HALVES) - 1:
                        count_end(psum[6])
                elif n == len(TURN_HALVES):
                    pe.wait_ge(const, 4)
                    for q in range(2):
                        pe.transpose(psum[5][:, q * P:(q + 1) * P], mask[:, q * P:(q + 1) * P], ident[:, :]).then_inc(setup_mm, 1)

            sort_turns(0, requests)
            tile_blocks(0)

            for layer in range(2):
                pe.wait_ge(sorted_ready, layer + 1)
                with pe.Fori(0, groups_of(pe, layer)) as i:
                    most = pe.value_load(gspan[0:1, bass.ds(i, 1)], min_val=0, max_val=BLOCKS)
                    with pe.If(most >= W):
                        for u in range(TG):
                            pe.wait_ge(gathered[u], (i + (layer * GROUPS + 1)) * 16)
                        pe.sem_inc(held, 1)
                        with pe.Fori(0, TG) as u:
                            s = pe.value_load(span[0:1, bass.ds(i * TG + u, 1)], min_val=0, max_val=BLOCKS)
                            with pe.If(s >= W):
                                with pe.Fori(W, s + 1) as j:
                                    visits.add()
                                    pe.wait_ge(x_oh, visits.value())
                                    for a in range(PARTS):
                                        mm = pe.matmul(psum[4][:, 0:F], xoh[:, :],
                                                       ring[:, :, :].rearrange("p u f -> p (u f)")[:, bass.ds(u * ROW + a * F, F)],
                                                       start=(a == 0), stop=(a == PARTS - 1))
                                    mm.then_inc(x_mm, 1)
                                pe.nop()
                            pe.nop()
                        pe.nop()
                    for u in range(TG):
                        if u % HT == 0:
                            pe.wait_ge(oh_ready, (i + layer * GROUPS) * 2 + (u // HT + 1))
                        pe.wait_ge(gathered[u], (i + (layer * GROUPS + 1)) * 16)
                        pe.wait_ge(added, (i + layer * GROUPS) * TG + (u + 1))
                        for w in range(W):
                            for a in range(PARTS):
                                mm = pe.matmul(psum[u % NPS][:, w * F:(w + 1) * F],
                                               ohw[:, w * P:(w + 1) * P, u % HT], ring[:, u, a * F:(a + 1) * F],
                                               start=(a == 0), stop=(a == PARTS - 1))
                        mm.then_inc(mm_done, 1)
                if layer == 0:
                    def node_rows(g):
                        pe.wait_ge(node_st, g * 3 + 1 + 1)
                        for q in range(BB // 2):
                            mm = pe.transpose(psum[5][:, q * P:(q + 1) * P], stage[:, q * P:(q + 1) * P], ident[:, :])
                        mm.then_inc(node_tr, 1)
                        pe.wait_ge(node_zt, g + 1)
                        for q in range(BB // 2):
                            mm = pe.matmul(psum[6][:, q * P:(q + 1) * P], zt[:, q * P:(q + 1) * P], w12[:, :],
                                           start=True, stop=True)
                        mm.then_inc(node_mm, 1)
                    node_rows(0)
                    sort_turns(1, lambda n: node_rows(n + 1))
                    tile_blocks(1)
                    pe.wait_ge(counts_in, 1)
                    pe.transpose(psum[7][0:1, 0:P], cnt[:, 0:1], ident[:, :]).then_inc(count_tr, 1)

        @block.vector
        def _(dve):
            visits = Count(dve, "dve_visits")
            chain = Count(dve, "dve_chain")
            blk_reg = dve.alloc_register("dve_block")
            at = [0]

            def note(ins):
                at[0] += 1
                ins.then_inc(step, 1)

            def link(ins):
                at[0] += 1
                ins.then_inc(step, 1)
                dve.wait_ge(step, at[0])

            def one_hots(parts, lanes, blocks, half, h, n):
                dve.wait_ge(hist_mm, n)
                both = ((oh[0:parts, h, 0:P * HT], lanes, P), (oh[0:parts, h, P * HT:], blocks, BLOCKS))
                for o, d, m in both[0 if lanes is not None else 1:]:
                    dve.tensor_tensor(o.rearrange("p (j t) -> p j t", t=HT), iorep[0:parts, 0:m, :],
                                      d[0:parts, bass.ds(half * HT, HT)].unsqueeze(1).to_broadcast([parts, m, HT]),
                                      ALU.is_equal).then_inc(hist_oh, 1)

            dve.sem_inc(added, FREE_PS)
            dve.sem_inc(flagged, 1)
            dve.sem_inc(taken, 1)
            link(dve.memset(acc[:, FULLB * F:], 0.0))
            dve.sem_inc(const, 1)

            dve.memset(zero[:, :], 0.0)
            dve.memset(w12[:, :], 0.0)
            dve.memset(zf[:, :], 0.0)
            dve.memset(ones[:, :], 1.0)
            dve.memset(mask[:, :], 0.0)
            dve.memset(deg[:, :], 1.0)
            link(dve.memset(k_b[:, :], PADKEY))
            dve.wait_ge(iotas, 3)
            dve.tensor_copy(colf[:, :], it_i[:, 0:P])
            link(dve.tensor_copy(rowf[:, :], it_y[:, 0:1]))
            link(dve.tensor_scalar(ident[:, :], colf[:, :], rowf[:, 0:1], None, ALU.is_equal))
            link(dve.tensor_copy(ident_h[:, :], ident[:, :]))
            dve.tensor_tensor(diff[:, 1:P], ident[:, 1:P], ident[:, 0:P - 1], ALU.subtract)
            link(dve.tensor_tensor(diff[:, 0:1], ident[:, 0:1], ident[:, P - 1:P], ALU.add))
            link(dve.tensor_scalar(xblk[:, :], it_i[:, 0:PADB], float(P), float(OFF * P), ALU.mult, ALU.add))
            dve.sem_inc(const, 1)
            dve.wait_ge(setup_mm, 1)
            dve.wait_ge(w_in, 64)
            dve.tensor_copy(w1t[:, 0:F], psum[6][:, 0:F])
            dve.tensor_scalar(b1r[:, :], zf[:, :], b1s[:, 0:1], None, ALU.add)
            link(dve.tensor_copy(w1t[:, F:2 * F], psum[6][:, 0:F]))
            dve.sem_inc(const, 1)
            dve.wait_ge(setup_mm, 3)
            dve.tensor_copy(w12[0:F, 0:F], psum[5][0:F, 0:F])
            dve.tensor_copy(w12[F:2 * F, F:2 * F], psum[5][F:2 * F, 0:F])
            link(dve.tensor_copy(c12[:, :], psum[4][:, 0:F]))

            dve.wait_ge(req_in, 16)
            reqf, reqn = k_a[:, 0:RT], k_a[:, RT:2 * RT]
            link(dve.tensor_copy(reqf, req[:, :]))
            link(dve.tensor_scalar(reqn, reqf, 0.0, float(NODES), ALU.is_lt, ALU.mult))
            link(dve.tensor_tensor(reqf, reqf, reqn, ALU.add))
            link(dve.tensor_scalar(req[:, :], reqf, 0.0, float(NODES - 1), ALU.max, ALU.min))

            low = k_a[:, 0:RT].bitcast(I32)
            link(dve.tensor_scalar(low, req[:, :], P - 1, None, ALU.bitwise_and))
            link(dve.tensor_copy(rlo, low))
            link(dve.tensor_scalar(low, req[:, :], 7, None, ALU.logical_shift_right))
            link(dve.tensor_copy(rhi, low))
            with dve.Fori(0, R0 // 2) as i:
                for h in range(2):
                    one_hots(P, rlo, rhi, i * 2 + h, h, i * 2 + (h + 1))

            dve.wait_ge(edge_in, 32)
            low = k_a[0:EP, 0:EC].bitcast(I32)
            link(dve.tensor_scalar(low, dst_raw, P - 1, None, ALU.bitwise_and))
            link(dve.tensor_copy(dlo, low))
            link(dve.tensor_scalar(nlo, low, -1.0, 0.5, ALU.mult, ALU.add))
            dve.sem_inc(nlo_ready, 1)
            link(dve.tensor_scalar(low, dst_raw, 7, None, ALU.logical_shift_right))
            link(dve.tensor_copy(dhi, low))
            with dve.Fori(0, HALVES // HU) as i:
                for m in range(HU):
                    one_hots(EP, None if m % 3 == 2 else dlo, dhi, i * HU + m, m % 2, i * HU + (m + 1 + R0))

            dve.wait_ge(counted, 2)
            link(dve.tensor_copy(stepsum[:, :], psum[5][:, 0:BLOCKS]))
            dve.sem_inc(deg_steps, 1)
            link(dve.tensor_scalar(deg[:, 0:BLOCKS], psum[7][:, 0:BLOCKS], 1.0, None, ALU.add))
            dve.wait_ge(setup_mm, 4)
            link(dve.scalar_tensor_tensor(out=deg[:, 0:BLOCKS], in0=psum[4][:, 0:BLOCKS], scalar=0.5, in1=deg[:, 0:BLOCKS],
                                          op0=ALU.mult, op1=ALU.add))
            dve.sem_inc(deg_ready, 1)

            link(dve.tensor_scalar(odd_i[:, :], it_y[:, 0:1], 1, None, ALU.bitwise_and))
            link(dve.tensor_copy(odd[:, :], odd_i[:, :]))
            dve.wait_ge(iotas, 3 + SB)
            link(dve.tensor_scalar(sgn_t[:, 6, :], sgn_t[:, 6, :], odd[:, 0:1], None, ALU.add))
            for sgn in (sgn_t, sgn_l):
                link(dve.tensor_scalar(sgn[:, :, :], sgn[:, :, :], 1.0, -2.0, ALU.is_equal, ALU.mult))
                link(dve.tensor_scalar(sgn[:, :, :], sgn[:, :, :], 1.0, None, ALU.add))

            dve.wait_ge(root, 1)
            link(dve.reciprocal(dinv[:, :], nwt[:, :]))
            link(dve.tensor_tensor(nwt[:, :], dinv[:, :], dinv[:, :], ALU.mult))
            link(dve.tensor_tensor(nwt[:, :], nwt[:, :], deg[:, :], ALU.mult))
            link(dve.tensor_scalar(nwt[:, :], nwt[:, :], -0.5, 1.5, ALU.mult, ALU.add))
            link(dve.tensor_tensor(dinv[:, :], dinv[:, :], nwt[:, :], ALU.mult))

            dve.wait_ge(emb_in, 32)
            link(dve.tensor_tensor(acc3, acc3, dinv[:, :].unsqueeze(2).to_broadcast([P, PADB, F]), ALU.mult))
            dve.sem_inc(scaled, 1)

            up = k_a[0:EP, 0:EC].bitcast(I32)
            link(dve.tensor_scalar(up, dst_raw, float(OFF * P), None, ALU.add))
            link(dve.tensor_scalar(dst_raw, up, KSHIFT, None, ALU.logical_shift_left))
            link(dve.tensor_tensor(k_b[0:EP, :].bitcast(I32).rearrange("p (c j) -> p c j", j=COLS)[:, :, 0:CE],
                                   dst_raw.rearrange("p (c j) -> p c j", j=CE),
                                   src_raw.rearrange("p (c j) -> p c j", j=CE), ALU.bitwise_or))

            def signed(src, dst, k):
                a, b = (x.rearrange("p (g j) -> p g j", j=P) for x in (src, dst))
                dve.tensor_tensor(b, a, sgn_t[:, k:k + 1, :].to_broadcast([P, ALL // P, P]), ALU.mult).then_inc(k_stage, 1)

            def exchange(src, dst, stride):
                a, b = (x.rearrange("p (g t s) -> p g t s", t=2, s=stride) for x in (src, dst))
                dve.tensor_tensor(b[:, :, 0, :], a[:, :, 0, :], a[:, :, 1, :], ALU.min).then_inc(k_stage, 1)
                dve.tensor_tensor(b[:, :, 1, :], a[:, :, 0, :], a[:, :, 1, :], ALU.max).then_inc(k_stage, 1)

            def b3(x):
                return x.rearrange("p (b f) -> p b f", f=F)

            def node_stage(g):
                wait_if(dve, node_mm, g)
                d3 = dinv[:, g * BB:(g + 1) * BB].unsqueeze(2).to_broadcast([P, BB, F])
                dve.tensor_tensor(b3(stage), acc3[:, g * BB:(g + 1) * BB, :], d3, ALU.mult).then_inc(node_st, 1)

            def node_next(g):
                d3 = dinv[:, g * BB:(g + 1) * BB].unsqueeze(2).to_broadcast([P, BB, F])
                dve.wait_ge(node_mm, g + 1)
                dve.tensor_tensor(b3(tnode), b3(psum[6][:, :]), c12[:, :].unsqueeze(1).to_broadcast([P, BB, F]), ALU.add).then_inc(node_st, 1)
                dve.wait_ge(node_st, g * 3 + 3)
                dve.tensor_tensor(acc3[:, g * BB:(g + 1) * BB, :], b3(tnode), d3, ALU.mult).then_inc(node_st, 1)

            def requests(n):
                if n < len(TURN_HALVES):
                    for m in range(sum(TURN_HALVES[:n]), sum(TURN_HALVES[:n + 1])):
                        one_hots(P, rlo, rhi, R0 + m, m % 2, R0 + HALVES + m + 1)
                else:
                    dve.wait_ge(counted, 3)
                    link(dve.tensor_scalar(mask[:, 0:BLOCKS], psum[6][:, 0:BLOCKS], 1.0, None, ALU.min))
                    dve.sem_inc(const, 1)
                    a, b = sdst[:, 0:RT], sdst[:, RT:2 * RT]
                    link(dve.tensor_scalar(a, io_r[:, :], -1.0, float(RT - 1 + (1 << 15)), ALU.mult, ALU.add))
                    link(dve.tensor_scalar(b, a, KSHIFT, None, ALU.logical_shift_left))
                    link(dve.tensor_tensor(a, b, req[:, :], ALU.bitwise_or))
                    link(dve.tensor_scalar(b.bitcast(F32), req[:, :], float(LAST), None, ALU.is_lt))
                    link(dve.tensor_tensor(reqkey[:, :], a.bitcast(F32), b.bitcast(F32), ALU.mult))
                    link(dve.tensor_scalar(pbase[:, :], rowf[:, :], float(RT), float(RT - 1), ALU.mult, ALU.add))

            def sort(rnd, nodes_too):
                n = 0
                due = None
                for what, k, src, dst, before in steps:
                    if before:
                        dve.wait_ge(k_stage, rnd * SORT_STEPS + before)
                    if what == "sign":
                        signed(src, dst, k)
                    elif what == "exchange":
                        exchange(src, dst, k)
                        if due is not None:
                            node_next(due)
                            due = None
                    else:
                        if nodes_too:
                            node_stage(n + 1)
                            due = n + 1
                        else:
                            requests(n)
                        n += 1
                        if what == "from_l":
                            for c in range(CHUNKS):
                                dve.wait_ge(tr_l, rnd * TO_L + (k - 8) * CHUNKS + c + 1)
                                dve.tensor_tensor(dst[:, c * COLS:(c + 1) * COLS], psum[c][:, 0:COLS],
                                                  sgn_l[:, k - 8, :], ALU.mult).then_inc(ev_l, 1)
                            dve.wait_ge(ev_l, rnd * TO_L + (k - 7) * CHUNKS)
                        else:
                            dve.wait_ge(ev_t, rnd * EV_T + (k - 7) * CHUNKS)
                rows = TILES // CHUNKS

                def by_tile(x):
                    return x.rearrange("p (r c) -> p r c", c=CHUNKS)

                def by_row(x):
                    return x.rearrange("p (c j) -> p j c", c=CHUNKS)[:, 0:rows, :]

                dve.wait_ge(k_stage, (rnd + 1) * SORT_STEPS)
                if nodes_too:
                    node_stage(n + 1)
                link(dve.tensor_scalar(by_tile(sidx[:, :]), by_row(final.bitcast(I32)), (1 << KSHIFT) - 1, None, ALU.bitwise_and))
                if not nodes_too:
                    dve.sem_inc(sources_ready, 1)
                    dve.wait_ge(setup_mm, 6)
                    link(dve.tensor_copy(maskt[:, :, :].rearrange("p n j -> p (n j)"), psum[5][:, 0:2 * P]))
                    dve.sem_inc(const, 1)
                link(dve.tensor_copy(by_tile(skey.bitcast(F32)), by_row(final)))
                dve.sem_inc(keys_read, 1)
                if nodes_too:
                    node_next(n + 1)
                per = COLS // P
                for c in range(CHUNKS):
                    dve.wait_ge(tr_t, (rnd + 1) * TO_T - CHUNKS + c + 1)
                    for e, op in enumerate((ALU.min, ALU.max)):
                        note(dve.tensor_reduce(ends[:, e, c * per:(c + 1) * per], psum[c][:, :].rearrange("p (q l) -> p q l", l=P), AX.X, op))
                link(dve.tensor_scalar(sdst, skey, KSHIFT, None, ALU.logical_shift_right))
                link(dve.tensor_scalar(ends_i[:, :, :], ends[:, :, :].bitcast(I32), KSHIFT + 7, None, ALU.logical_shift_right))
                note(dve.tensor_scalar(ends_b[:, 0, :], ends_i[:, 0, :], float(BLOCKS + OFF), None, ALU.min))
                link(dve.tensor_scalar(ends_b[:, 1, :], ends_i[:, 1, :], float(BLOCKS - 1 + OFF), None, ALU.min))
                dve.sem_inc(prep, 1)
                if nodes_too:
                    for c in range(CHUNKS):
                        dve.wait_ge(bc, (2 * rnd) * CHUNKS + c + 1)
                        note(dve.tensor_reduce(vrow[:, c, :], psum[c][0:1, 0:rows].rearrange("p (g r) -> p g r", g=GROUPS), AX.X, ALU.min))
                    dve.wait_ge(step, at[0])
                    link(dve.tensor_reduce(vgrp[:, :], vrow[:, :, :].rearrange("p c g -> p g c"), AX.X, ALU.min))
                    link(dve.tensor_scalar(vgrp[:, :], vgrp[:, :], float(BLOCKS + OFF), None, ALU.is_lt))
                    link(dve.tensor_reduce(vsum[:, :], vgrp[:, :], AX.X, ALU.add))
                    link(dve.tensor_scalar(ngrp[:, :], vsum[:, :], 1.0, None, ALU.max))
                    dve.sem_inc(sources_ready, 1)
                for c in range(CHUNKS):
                    dve.wait_ge(bc, (2 * rnd) * CHUNKS + c + 1)
                    note(dve.tensor_scalar(by_tile(blo[0:1, :])[:, :, c], psum[c][0:1, 0:rows], float(-OFF), float(BLOCKS - 1), ALU.add, ALU.min))
                    dve.scalar_tensor_tensor(out=by_tile(rel)[:, :, c], in0=psum[c][:, 0:rows], scalar=float(-P),
                                             in1=by_tile(sdst)[:, :, c], op0=ALU.mult, op1=ALU.add).then_inc(prep, 1)
                dve.wait_ge(step, at[0])
                dve.wait_ge(prep, (rnd + 1) * (1 + CHUNKS))
                for c in range(CHUNKS):
                    dve.wait_ge(bc, (2 * rnd + 1) * CHUNKS + c + 1)
                    note(dve.scalar_tensor_tensor(out=by_tile(span[0:1, :])[:, :, c], in0=psum[c][0:1, 0:rows], scalar=float(-OFF),
                                                  in1=by_tile(blo[0:1, :])[:, :, c], op0=ALU.add, op1=ALU.subtract))
                dve.wait_ge(step, at[0])
                link(dve.tensor_reduce(gspan[0:1, :], span[0:1, :].rearrange("p (g t) -> p g t", t=TG), AX.X, ALU.max))
                dve.sem_inc(sorted_ready, 1)

            sort(0, False)

            for layer in range(2):
                base = layer * GROUPS
                if layer == 0:
                    dve.wait_ge(wanted_in, 16)
                with dve.Fori(0, groups_of(dve, layer)) as i:
                    most = dve.value_load(gspan[0:1, bass.ds(i, 1)], min_val=0, max_val=BLOCKS)
                    with dve.If(most >= W):
                        dve.wait_ge(added, (i + base) * TG + FREE_PS)
                        dve.sem_inc(held, 1)
                        with dve.Fori(0, TG) as u:
                            s = dve.value_load(span[0:1, bass.ds(i * TG + u, 1)], min_val=0, max_val=BLOCKS)
                            with dve.If(s >= W):
                                first = dve.value_load(blo[0:1, bass.ds(i * TG + u, 1)], min_val=0, max_val=BLOCKS - 1)
                                chain.add()
                                dve.tensor_scalar(xdst[:, :], skey[:, bass.ds(i * TG + u, 1)], KSHIFT, None,
                                                  ALU.logical_shift_right).then_inc(x_chain, 1)
                                dve.wait_ge(x_chain, chain.value())
                                chain.add()
                                dve.tensor_copy(xdsf[:, :], xdst[:, :]).then_inc(x_chain, 1)
                                dve.wait_ge(x_chain, chain.value())
                                dve.sem_inc(held, 1)
                                with dve.Fori(W, s + 1) as j:
                                    visits.add()
                                    dve.reg_add(blk_reg, first, j)
                                    at_blk = dve.snap(blk_reg, min_val=0, max_val=BLOCKS - 1)
                                    dve.tensor_scalar(xoh[:, :], colf[:, :], xblk[:, bass.ds(at_blk, 1)], xdsf[:, 0:1],
                                                      ALU.add, ALU.is_equal).then_inc(x_oh, 1)
                                    dve.wait_ge(x_mm, visits.value())
                                    rows_of = acc[:, bass.ds(at_blk * F, F)]
                                    chain.add()
                                    dve.tensor_tensor(rows_of, psum[4][:, 0:F], rows_of, ALU.add).then_inc(x_chain, 1)
                                    dve.wait_ge(x_chain, chain.value())
                                dve.nop()
                            dve.nop()
                        dve.nop()
                    for u in range(TG):
                        if u % HT == 0:
                            if layer == 0:
                                dve.wait_ge(flagged, i * TG + (u + 1))
                            dve.tensor_tensor(ohw, iorep[:, :, :],
                                              rel[:, bass.ds(i * TG + u, HT)].unsqueeze(1).to_broadcast([P, W * P, HT]),
                                              ALU.is_equal).then_inc(oh_ready, 1)
                            firsts = load_row(dve, blo[0:1, bass.ds(i * TG + u, HT)], BLOCKS - 1)
                        if layer == 0 and u == 4:
                            dve.wait_ge(taken, i * 2 + 1)
                            dve.wait_ge(comp_done, i + 1)
                            dve.sem_inc(held, 1)
                            dve.max(top8[:, :], reqkey[:, :]).then_inc(taken, 1)
                        if layer == 0 and u == 8:
                            dve.wait_ge(taken, i * 2 + 2)
                            dve.sem_inc(held, 1)
                            dve.match_replace(reqkey[:, :], top8[:, :], reqkey[:, :], 0.0).then_inc(taken, 1)
                        first = firsts[u % HT]
                        dve.wait_ge(mm_done, (i + base) * TG + (u + 1 + FREE_MM))
                        dve.wait_ge(added, (i + base) * TG + (u + FREE_PS))
                        window = acc[:, bass.ds(first * F, W * F)]
                        dve.tensor_tensor(window, psum[u % NPS][:, 0:W * F], window, ALU.add).then_inc(added, 1)
                        if layer == 0:
                            dve.wait_ge(flagged, i * TG + (u + 1))
                            dve.scalar_tensor_tensor(
                                out=junk[:, :], in0=ohw[:, :, u % HT], scalar=1.0,
                                in1=wanted[:, bass.ds(first * P, W * P)], op0=ALU.mult, op1=ALU.mult,
                                accum_out=keep[:, bass.ds(i * TG + u, 1)]).then_inc(flagged, 1)

                if layer == 0:
                    dve.wait_ge(added, GROUPS * TG + FREE_PS)
                    dve.wait_ge(flagged, GROUPS * TG + 1)
                    dve.sem_inc(node_st, 1)
                    far = k_a[:, 0:TILES]
                    node_stage(0)
                    link(dve.tensor_scalar(far, rel, float(W * P), None, ALU.is_ge))
                    link(dve.tensor_tensor(keep[:, :], keep[:, :], far, ALU.max))
                    link(dve.memset(k_b, PADKEY))
                    link(dve.copy_predicated(k_b.rearrange("p (c j) -> p j c", c=CHUNKS)[:, 0:TILES // CHUNKS, :],
                                             keep[:, :].bitcast(I32).rearrange("p (j c) -> p j c", c=CHUNKS),
                                             skey.bitcast(F32).rearrange("p (j c) -> p j c", c=CHUNKS)))
                    node_next(0)
                    sort(1, True)

                    dve.wait_ge(comp_done, GROUPS + 1)
                    cb = comp[:, 0:RCOLS].bitcast(I32)
                    t0, t1 = k_a[:, 0:RCOLS], k_a[:, RCOLS:2 * RCOLS]
                    link(dve.tensor_scalar(ccol[:, 0, :], cb, (1 << KSHIFT) - 1, None, ALU.bitwise_and))
                    link(dve.tensor_scalar(t0.bitcast(I32), cb, KSHIFT, 1023, ALU.logical_shift_right, ALU.bitwise_and))
                    link(dve.tensor_scalar(t1, t0.bitcast(I32), -1.0, pbase[:, 0:1], ALU.mult, ALU.add))
                    link(dve.tensor_scalar(t0, comp[:, 0:RCOLS], 0.0, float(1 << 20), ALU.is_equal, ALU.mult))
                    link(dve.tensor_tensor(ccol[:, 1, :], t0, t1, ALU.add))
                    link(dve.tensor_scalar(t0, comp[:, 0:RCOLS], 0.0, None, ALU.is_gt))
                    link(dve.tensor_reduce(cnt[:, :], t0, AX.X, ALU.add))
                    dve.sem_inc(counts_in, 1)
                    dve.wait_ge(count_tr, 1)
                    link(dve.tensor_reduce(nrf[:, 0:1], psum[7][0:1, 0:P], AX.X, ALU.max))
                    link(dve.tensor_copy(nreq[:, 0:1], nrf[:, 0:1]))
                    link(dve.tensor_scalar(nrf[:, 1:1 + RCOLS // ROUND], io_r[0:1, 0:RCOLS // ROUND], float(ROUND), nrf[:, 0:1],
                                           ALU.mult, ALU.is_lt))
                    link(dve.tensor_reduce(nrf[:, 7:8], nrf[:, 1:1 + RCOLS // ROUND], AX.X, ALU.add))
                    link(dve.tensor_scalar(nreq[:, 1:2], nrf[:, 7:8], 1.0, None, ALU.max))
                    dve.sem_inc(counts, 1)

            dve.wait_ge(added, (groups_of(dve, 1) + GROUPS) * TG + FREE_PS)
            for n, (blk0, blk1) in enumerate([(FULLB, BLOCKS)] + PIECES):
                m = blk1 - blk0
                if n == 1:
                    dve.wait_ge(last_in, 16)
                    link(dve.tensor_copy(fill.rearrange("p (t f) -> p t f", f=F), lrow[:, :].unsqueeze(1).to_broadcast([P, FILL, F])))
                    dve.sem_inc(fill_ready, 1)
                link(dve.tensor_tensor(acc3[:, blk0:blk1, :], acc3[:, blk0:blk1, :], dinv[:, blk0:blk1].unsqueeze(2).to_broadcast([P, m, F]), ALU.mult))
                link(dve.tensor_tensor(acc3[:, blk0:blk1, :], acc3[:, blk0:blk1, :], b2r[:, :].unsqueeze(1).to_broadcast([P, m, F]), ALU.add))
                dve.sem_inc(rows_ready, 1)


_INS = ["r_input", "L0_rec_emb", "L0_rec_W1", "L0_rec_b1", "L0_rec_W2", "L0_rec_b2", "L0_rec_edge_index"]


def kernel(**inputs):
    import numpy as np
    import concourse.bacc as bacc
    from concourse.bass_utils import run_bass_kernel_spmd

    nc = bacc.Bacc("TRN2", target_bir_lowering=False, num_devices=1)
    arrays, args = {}, []
    for name in _INS:
        a = np.ascontiguousarray(inputs[name])
        arrays["in_" + name] = a
        args.append(nc.dram_tensor("in_" + name, a.shape, mybir.dt.from_np(a.dtype), kind="ExternalInput").ap())
    out = nc.dram_tensor("out", (BATCH, SEQ, F), F32, kind="ExternalOutput").ap()
    gcn_program(nc, *args, out)
    r = run_bass_kernel_spmd(nc, [arrays], core_ids=[0])
    return r.results[0]["out"]
```
